# Optimizing a Trainium2 kernel written in Bass

```python
import numpy as np
import jax
import jax.numpy as jnp

def _softmax(x, axis=-1):
    return jax.nn.softmax(x, axis=axis)

def _gelu(x):
    return jax.nn.gelu(x, approximate=True)

def _silu(x):
    return jax.nn.silu(x)

def _sigmoid(x):
    return jax.nn.sigmoid(x)

def _layernorm(x, axis=-1, eps=1e-05):
    m = jnp.mean(x, axis=axis, keepdims=True)
    v = jnp.var(x, axis=axis, keepdims=True)
    return (x - m) / jnp.sqrt(v + eps)

def _scatter_add(tgt, idx, src, axis=0):
    return tgt.at[idx].add(src)

def _segment_sum(src, seg, n):
    return jax.ops.segment_sum(src, seg, n)
kernel_name = 'mk_gnn_preln_d4_gnn_r8_134367'

def setup_inputs(seed: int=0):
    np.random.seed(seed)
    _w = jnp.asarray

    def _rec_inputs():
        import jax
        import jax.numpy as jnp
        _gk = jax.random.key(seed)
        x = -0.000202 + 1 * jax.random.normal(jax.random.fold_in(_gk, 1), (12500, 64), jnp.float32)
        src = jax.random.randint(jax.random.fold_in(_gk, 2), (400000,), 0, 12500, jnp.int32)
        dst = jax.random.randint(jax.random.fold_in(_gk, 3), (400000,), 0, 12500, jnp.int32)
        _o = jnp.argsort(dst, stable=True)
        src = src[_o]
        dst = dst[_o]
        edge_attr_64 = 9.41057e-06 + 1 * jax.random.normal(jax.random.fold_in(_gk, 12), (400000, 64), jnp.float32)
        edge_type_8 = jax.random.randint(jax.random.fold_in(_gk, 14), (400000,), 0, 8, jnp.int32)
        edge_weight = jax.random.uniform(jax.random.fold_in(_gk, 15), (400000,), jnp.float32, 0.0, 0.999999)
        edge_weight1 = jax.random.uniform(jax.random.fold_in(_gk, 16), (400000, 1), jnp.float32, 0.0, 0.999998)
        node_vec1 = jax.random.uniform(jax.random.fold_in(_gk, 17), (12500, 1), jnp.float32, 0.0, 0.999993)
        node_vec1_n2 = jax.random.uniform(jax.random.fold_in(_gk, 18), (12500, 1), jnp.float32, 0.0, 0.999993)
        return (x, src, dst, edge_attr_64, edge_type_8, edge_weight, edge_weight1, node_vec1, node_vec1_n2)
    x, src, dst, edge_attr_64, edge_type_8, edge_weight, edge_weight1, node_vec1, node_vec1_n2 = _rec_inputs()

    def _L0_gnn_setup():
        import jax, jax.numpy as jnp
        import numpy as np
        N_NODES = 12500
        N_EDGES = 200000
        D_FEAT = 64
        key = jax.random.key(seed)
        k1, k2 = jax.random.split(key)
        x = jax.random.normal(k1, (N_NODES, D_FEAT), dtype=jnp.float32)
        edge_index = jax.random.randint(k2, (2, N_EDGES), 0, N_NODES, dtype=jnp.int64)
        return {'x': x, 'edge_index': edge_index}
    _L0_gnn_all = _L0_gnn_setup()
    _L0_gnn_in = {k: v for k, v in _L0_gnn_all.items() if k in ()}
    del _L0_gnn_all

    def _L1_gnn_setup():
        import jax, jax.numpy as jnp
        import numpy as np
        N, E, R, D_IN, D_OUT = (6250, 100000, 8, 64, 64)
        key = jax.random.key(seed)
        ks = jax.random.split(key, 8)
        feat = jax.random.normal(ks[0], (N, D_IN), dtype=jnp.float32)
        edge_src = jax.random.randint(ks[1], (E,), 0, N, dtype=jnp.int32)
        edge_dst = jax.random.randint(ks[2], (E,), 0, N, dtype=jnp.int32)
        etype = jax.random.randint(ks[3], (E,), 0, R, dtype=jnp.int32)
        attention = jax.random.uniform(ks[4], (E, 1), dtype=jnp.float32)
        weight = jax.random.normal(ks[5], (R, D_IN, D_OUT), dtype=jnp.float32) * (6.0 / (D_IN + D_OUT)) ** 0.5
        h_bias = jnp.zeros((D_OUT,), dtype=jnp.float32)
        loop_weight = jax.random.normal(ks[6], (D_IN, D_OUT), dtype=jnp.float32) * (6.0 / (D_IN + D_OUT)) ** 0.5
        return {'feat': feat, 'edge_src': edge_src, 'edge_dst': edge_dst, 'etype': etype, 'attention': attention, 'weight': weight, 'h_bias': h_bias, 'loop_weight': loop_weight}
    _L1_gnn_all = _L1_gnn_setup()
    _L1_gnn_in = {k: v for k, v in _L1_gnn_all.items() if k in ('weight', 'h_bias', 'loop_weight')}
    del _L1_gnn_all

    def _L2_gnn_setup():
        import jax, jax.numpy as jnp
        import numpy as np

        def _gcn_norm(edge_index, edge_weight, num_nodes):
            loop = jnp.arange(num_nodes, dtype=edge_index.dtype)
            row = jnp.concatenate([edge_index[0], loop])
            col = jnp.concatenate([edge_index[1], loop])
            w = jnp.concatenate([edge_weight, jnp.ones((num_nodes,), edge_weight.dtype)])
            deg = jax.ops.segment_sum(w, col, num_segments=num_nodes)
            dinv = jnp.where(deg > 0, jax.lax.rsqrt(deg), 0.0).astype(edge_weight.dtype)
            norm = dinv[row] * w * dinv[col]
            return (row, col, norm)

        def sgc_forward(x, edge_index, edge_weight, W, b, K=2):
            n = x.shape[0]
            row, col, norm = _gcn_norm(edge_index, edge_weight, n)
            for _ in range(K):
                x = jax.ops.segment_sum(norm[:, None] * x[row], col, num_segments=n)
            out = x @ W.T + b
            return jax.nn.elu(out)
        key = jax.random.key(seed)
        k1, k2, k3, k4, k5 = jax.random.split(key, 5)
        N, E, F_IN, F_OUT = (6250, 156250, 64, 64)
        x = jax.random.normal(k1, (N, F_IN), dtype=jnp.float32)
        edge_index = jax.random.randint(k2, (2, E), 0, N, dtype=jnp.int64)
        edge_weight = jax.random.uniform(k3, (E,), dtype=jnp.float32)
        W = jax.random.normal(k4, (F_OUT, F_IN), dtype=jnp.float32) / np.sqrt(F_IN)
        b = jax.random.normal(k5, (F_OUT,), dtype=jnp.float32) * 0.01
        return {'x': x, 'edge_index': edge_index, 'edge_weight': edge_weight, 'W': W, 'b': b}
    _L2_gnn_all = _L2_gnn_setup()
    _L2_gnn_in = {k: v for k, v in _L2_gnn_all.items() if k in ('W', 'b')}
    del _L2_gnn_all

    def _L3_gnn_setup():
        import jax, jax.numpy as jnp
        import numpy as np
        N = 12500
        E = 400000
        D = 64
        key = jax.random.key(seed)
        k = jax.random.split(key, 7)
        weight = jax.random.normal(k[0], (N, D), dtype=jnp.float32) * 0.05
        ps_w = jax.random.normal(k[1], (1, D), dtype=jnp.float32) * 0.1
        review_feat = jax.random.normal(k[2], (E, D), dtype=jnp.float32)
        cj = jax.random.uniform(k[3], (N, 1), dtype=jnp.float32)
        ci = jax.random.uniform(k[4], (N, 1), dtype=jnp.float32)
        src = jax.random.randint(k[5], (E,), 0, N, dtype=jnp.int32)
        dst = jax.random.randint(k[6], (E,), 0, N, dtype=jnp.int32)
        return {'weight': weight, 'ps_w': ps_w, 'review_feat': review_feat, 'cj': cj, 'ci': ci, 'src': src, 'dst': dst}
    _L3_gnn_all = _L3_gnn_setup()
    _L3_gnn_in = {k: v for k, v in _L3_gnn_all.items() if k in ('ps_w',)}
    del _L3_gnn_all
    return {'x': x, 'src': src, 'dst': dst, 'edge_attr_64': edge_attr_64, 'edge_type_8': edge_type_8, 'edge_weight': edge_weight, 'edge_weight1': edge_weight1, 'node_vec1': node_vec1, 'node_vec1_n2': node_vec1_n2, 'L1_gnn_weight': _L1_gnn_in['weight'], 'L1_gnn_h_bias': _L1_gnn_in['h_bias'], 'L1_gnn_loop_weight': _L1_gnn_in['loop_weight'], 'L2_gnn_W': _L2_gnn_in['W'], 'L2_gnn_b': _L2_gnn_in['b'], 'L3_gnn_ps_w': _L3_gnn_in['ps_w']}

def reference(x, src, dst, edge_attr_64, edge_type_8, edge_weight, edge_weight1, node_vec1, node_vec1_n2, L1_gnn_weight, L1_gnn_h_bias, L1_gnn_loop_weight, L2_gnn_W, L2_gnn_b, L3_gnn_ps_w):
    import jax
    import jax.numpy as jnp

    def _L0_gnn_ref(x, edge_index):
        import jax, jax.numpy as jnp
        import numpy as np
        N_NODES = 12500
        N_EDGES = 200000
        D_FEAT = 64
        msgs = x[edge_index[0]]
        out = jax.ops.segment_sum(msgs, edge_index[1], num_segments=x.shape[0])
        return out

    def _L1_gnn_ref(feat, edge_src, edge_dst, etype, attention, weight, h_bias, loop_weight):
        import jax, jax.numpy as jnp
        import numpy as np
        N, E, R, D_IN, D_OUT = (6250, 100000, 8, 64, 64)
        proj = jnp.einsum('ni,rio->rno', feat, weight)
        m = (proj[etype, edge_src] + h_bias) * attention
        agg = jax.ops.segment_sum(m, edge_dst, num_segments=feat.shape[0])
        return agg + feat @ loop_weight

    def _L2_gnn_ref(x, edge_index, edge_weight, W, b):
        import jax, jax.numpy as jnp
        import numpy as np

        def _gcn_norm(edge_index, edge_weight, num_nodes):
            loop = jnp.arange(num_nodes, dtype=edge_index.dtype)
            row = jnp.concatenate([edge_index[0], loop])
            col = jnp.concatenate([edge_index[1], loop])
            w = jnp.concatenate([edge_weight, jnp.ones((num_nodes,), edge_weight.dtype)])
            deg = jax.ops.segment_sum(w, col, num_segments=num_nodes)
            dinv = jnp.where(deg > 0, jax.lax.rsqrt(deg), 0.0).astype(edge_weight.dtype)
            norm = dinv[row] * w * dinv[col]
            return (row, col, norm)

        def sgc_forward(x, edge_index, edge_weight, W, b, K=2):
            n = x.shape[0]
            row, col, norm = _gcn_norm(edge_index, edge_weight, n)
            for _ in range(K):
                x = jax.ops.segment_sum(norm[:, None] * x[row], col, num_segments=n)
            out = x @ W.T + b
            return jax.nn.elu(out)
        return sgc_forward(x, edge_index, edge_weight, W, b, K=2)

    def _L3_gnn_ref(weight, ps_w, review_feat, cj, ci, src, dst):
        import jax, jax.numpy as jnp
        import numpy as np
        N = 12500
        E = 400000
        D = 64
        feat = weight * cj
        pa = jax.nn.sigmoid(review_feat @ ps_w.T)
        msg = pa * feat[src]
        h = jax.ops.segment_sum(msg, dst, num_segments=weight.shape[0])
        return h * ci
    edge_index = jnp.stack([src, dst])
    h = jnp.maximum(_layernorm(x, axis=-1), 0.0)
    x = x + _L0_gnn_ref(h, edge_index)
    h = jnp.maximum(_layernorm(x, axis=-1), 0.0)
    x = x + _L1_gnn_ref(h, src, dst, edge_type_8, edge_weight1, L1_gnn_weight, L1_gnn_h_bias, L1_gnn_loop_weight)
    h = jnp.maximum(_layernorm(x, axis=-1), 0.0)
    x = x + _L2_gnn_ref(h, edge_index, edge_weight, L2_gnn_W, L2_gnn_b)
    h = jnp.maximum(_layernorm(x, axis=-1), 0.0)
    x = x + _L3_gnn_ref(h, L3_gnn_ps_w, edge_attr_64, node_vec1, node_vec1_n2, src, dst)
    return x

_drawn_inputs = setup_inputs


def setup_inputs(seed=0):
    import zlib

    import numpy as np

    out = dict(_drawn_inputs(seed))
    spreads = {'L1_gnn_h_bias': (0.0, 0.1)}
    factors = {'edge_attr_64': 3.472, 'edge_weight': 64.0, 'L2_gnn_b': 64.0, 'L3_gnn_ps_w': 3.295}
    for name, (base, spread) in spreads.items():
        noise = np.random.default_rng([zlib.crc32(name.encode()), seed]).standard_normal(out[name].shape)
        drawn = base * np.exp(spread * noise) if base else spread * noise
        out[name] = jnp.asarray(drawn.astype(out[name].dtype))
    for name, factor in factors.items():
        out[name] = (out[name] * factor).astype(out[name].dtype)
    return out
```

```python
import concourse.bass as bass
from concourse import mybir
from contextlib import ExitStack

N = 12500
E = 400000
D = 64
R = 8
P = 128
K = 5
GE = P * K
G = E // GE
U = 5
IT = G // U
NP = 125
NC = N // NP
C4 = 4
HOPS = 5
EPS = 1e-5

assert G * GE == E and IT * U == G and NP * NC == N and NC % C4 == 0


def gnn_kernel(nc, x, src, dst, etype, edge_attr, edge_w, att, cj, ci,
               rel_w, h_bias, loop_w, w_t, b2, ps_w, out):
    f32 = mybir.dt.float32
    i32 = mybir.dt.int32
    ALU = mybir.AluOpType
    ACT = mybir.ActivationFunctionType
    AX = mybir.AxisListType.X

    table = [nc.dram_tensor(f"table{h}", [R * N if h == 1 else N, D], f32).ap() for h in range(HOPS)]
    width = [D + 1 if h == 0 else D for h in range(HOPS)]
    agg = [nc.dram_tensor(f"agg{h}", [N + P, width[h]], f32).ap() for h in range(HOPS)]

    def by_node(ap):
        return ap.rearrange("(p c) f -> p c f", p=NP)

    ctx = ExitStack()
    with ctx:
        def sb(name, shape, dt=f32):
            return ctx.enter_context(nc.sbuf_tensor(name, shape, dt))

        def sem(name):
            return ctx.enter_context(nc.semaphore(name))

        xs = sb("xs", [NP, NC, D])
        hs = sb("hs", [NP, NC, D])
        wide = sb("wide", [P, NC * (D + 1)])
        deg = sb("deg", [NP, NC])
        dinv = sb("dinv", [NP, NC])
        dinv2 = sb("dinv2", [NP, NC])
        st1 = sb("st1", [NP, NC])
        st2 = sb("st2", [NP, NC])
        cj_sb = sb("cj_sb", [NP, NC])
        ci_sb = sb("ci_sb", [NP, NC])
        idx_src = sb("idx_src", [P, (G + U) * K], i32)
        idx_rel = sb("idx_rel", [P, (G + U) * K], i32)
        off = sb("off", [P, G * K])
        w_att = sb("w_att", [P, G * K])
        w_edge = sb("w_edge", [P, G * K])
        base = sb("base", [P, G + 1])
        delta = sb("delta", [P, G])
        carry_at = sb("carry_at", [P, G])
        base_row = sb("base_row", [1, G + 1])
        base_i = sb("base_i", [1, G], i32)
        idx_now = sb("idx_now", [P, U * K], i32)
        rows = sb("rows", [P, U, K, D + 1])
        pick = sb("pick", [P, K, P])
        carry = sb("carry", [P, U, P])
        summed = sb("summed", [P, U, D + 1])
        attr = sb("attr", [P, U, K * D])
        prod = sb("prod", [P, U * K, D])
        z25 = sb("z25", [P, U * K])
        stage = sb("stage", [NP, C4, D])
        h_t = sb("h_t", [D, C4 * NP])
        proj_sb = sb("proj_sb", [NP, R, C4, D])
        w_all = sb("w_all", [D, (R + 1) * D])
        w2_sb = sb("w2_sb", [D, D])
        hb_b = sb("hb_b", [NP, D])
        b2_b = sb("b2_b", [NP, D])
        ps_b = sb("ps_b", [P, D])
        iota_row = sb("iota_row", [P, P])
        iota_col = sb("iota_col", [P, 1])
        ident = sb("ident", [P, P])
        earlier = sb("earlier", [P, P])
        ones = sb("ones", [P, P])
        spare = sb("spare", [P, 1])
        mins = sb("mins", [P, 4])
        flag = sb("flag", [1, 1], i32)
        gidx = sb("gidx", [P, 1], i32)
        didx = sb("didx", [P, 1], i32)
        dcol = sb("dcol", [P, 2])
        diag = sb("diag", [P, P])
        same = sb("same", [P, P])
        same_w = sb("same_w", [P, P])
        grow = sb("grow", [P, D + 1])
        merged = sb("merged", [P, D + 1])

        bank = [ctx.enter_context(nc.psum_tensor(f"bank{b}", [P, 512], f32)) for b in range(8)]
        acc = bank[0:U]

        agg_sb = [wide[0:NP, 0:NC * width[h]].rearrange("p (c f) -> p c f", f=width[h]) for h in range(HOPS)]
        scratch = wide[0:NP, 0:NC * D].rearrange("p (c f) -> p c f", f=D)
        off_g = off[:, :].rearrange("p (g k) -> p g k", k=K)
        weights = [None, w_att, w_edge, w_edge, w_att]
        index = [idx_src, idx_rel, idx_src, idx_src, idx_src]

        attr_d = edge_attr.rearrange("(i u p k) f -> i p u (k f)", u=U, p=P, k=K)

        loaded = sem("loaded")
        consts = sem("consts")
        v = sem("v")
        a_out = sem("a_out")
        v_out = sem("v_out")
        base_f = sem("base_f")
        base_b = sem("base_b")
        ok_col = sem("ok_col")
        ok_sum = sem("ok_sum")
        setup = sem("setup")
        hop_ready = sem("hop_ready")
        table_out = sem("table_out")
        rows_ready = sem("rows_ready")
        table_ready = sem("table_ready")
        gathered = [sem(f"gathered{u}") for u in range(U)]
        idx_ready = sem("idx_ready")
        paced = sem("paced")
        pick_ready = sem("pick_ready")
        group_done = sem("group_done")
        evacuated = sem("evacuated")
        stored = sem("stored")
        summed_free = sem("summed_free")
        agg_ready = sem("agg_ready")
        agg_in = sem("agg_in")
        attr_in = sem("attr_in")
        attr_used = sem("attr_used")
        gate_ready = sem("gate_ready")
        staged = sem("staged")
        turned = sem("turned")
        h_t_ready = sem("h_t_ready")
        projected = sem("projected")
        proj_ready = sem("proj_ready")
        proj_free = sem("proj_free")
        banks_free = sem("banks_free")
        node_ready = sem("node_ready")
        z_ready = sem("z_ready")
        prod_ready = sem("prod_ready")
        act_paced = sem("act_paced")
        pe_paced = sem("pe_paced")
        proj_stored = sem("proj_stored")
        out_stored = sem("out_stored")
        g_zeroed = sem("g_zeroed")
        g_zeros = sem("g_zeros")
        g_idx = sem("g_idx")
        g_diag = sem("g_diag")
        g_dst = sem("g_dst")
        g_same = sem("g_same")
        g_rows = [sem(f"g_rows{h}") for h in range(HOPS)]
        g_sum = sem("g_sum")
        g_merged = sem("g_merged")
        g_scat = [sem(f"g_scat{h}") for h in range(HOPS)]
        g_start = sem("g_start")
        g_free = sem("g_free")
        g_v = sem("g_v")

        LOADS = 15
        STEPS = NC // C4
        TILES = G * K
        CHAIN = 7

        block = ctx.enter_context(nc.Block())

        @block.sync
        def _(sp):
            sp.dma_start(xs[:, :, :], by_node(x)).then_inc(loaded, 16)
            for to, of in ((idx_src[:, 0:G * K], src), (idx_rel[:, 0:G * K], etype),
                           (off[:, :].bitcast(i32), dst), (w_att[:, :], att), (w_edge[:, :], edge_w)):
                sp.dma_start(to, of).then_inc(loaded, 16)
            with nc.allow_non_contiguous_dma(reason="625 words, once"):
                sp.dma_start(base_i[0:1, :], dst.rearrange("p (g k) -> p k g", k=K)[0:1, 0, :]).then_inc(loaded, 16)
            sp.dma_start(cj_sb[:, :], cj.rearrange("(p c) o -> p (c o)", p=NP)).then_inc(loaded, 16)
            sp.dma_start(ci_sb[:, :], ci.rearrange("(p c) o -> p (c o)", p=NP)).then_inc(loaded, 16)
            sp.dma_start(w_all[:, 0:R * D].rearrange("i (r o) -> i r o", r=R),
                         rel_w.rearrange("r i o -> i r o")).then_inc(loaded, 16)
            sp.dma_start(w_all[:, R * D:], loop_w).then_inc(loaded, 16)
            sp.dma_start(w2_sb[:, :], w_t).then_inc(loaded, 16)
            sp.dma_start(hb_b[:, :], h_bias.rearrange("(a f) -> a f", a=1).to_broadcast([NP, D])).then_inc(loaded, 16)
            sp.dma_start(b2_b[:, :], b2.rearrange("(a f) -> a f", a=1).to_broadcast([NP, D])).then_inc(loaded, 16)
            sp.dma_start(ps_b[:, :], ps_w.to_broadcast([P, D])).then_inc(loaded, 16)
            sp.wait_ge(setup, 1)
            ok = sp.value_load(flag[0:1, 0:1], min_val=0, max_val=1)
            stores = 0
            for h in range(HOPS):
                if h == 1:
                    t1 = table[1].rearrange("(r p c) f -> p r c f", r=R, p=NP)
                    with sp.Fori(0, STEPS) as i:
                        sp.wait_ge(proj_ready, i + 1)
                        for r in range(R):
                            sp.dma_start(t1[:, r, bass.ds(i * C4, C4), :], proj_sb[:, r, :, :]).then_inc(proj_stored, 16)
                        sp.wait_ge(proj_stored, i * (16 * R) + 16 * R)
                        sp.sem_inc(proj_free, 1)
                else:
                    stores += 1
                    sp.wait_ge(rows_ready, stores)
                    sp.dma_start(by_node(table[h]), hs[:, :, :]).then_inc(table_out, 16)
                    sp.wait_ge(table_out, 16 * stores)
                sp.sem_inc(table_ready, 1)
                W = width[h]
                with sp.If(ok == 1):
                    with sp.Fori(0, IT) as i:
                        for u in range(U):
                            start = sp.value_load(base_i[0:1, bass.ds(i * U + u, 1)], min_val=0, max_val=N - 1)
                            sp.wait_ge(evacuated, i * U + (h * G + u + 2))
                            sp.dma_start(agg[h][bass.ds(start, P), :], summed[:, u, 0:W]).then_inc(stored, 16)
                            sp.wait_ge(stored, i * (16 * U) + 16 * (h * G + u + 1))
                            sp.sem_inc(summed_free, 1)
                with sp.Else():
                    sp.wait_ge(g_zeroed, h + 1)
                    zeros = wide[0:NP, 0:NC * W]
                    sp.dma_start(agg[h][0:N, :].rearrange("(p c) f -> p (c f)", p=NP), zeros).then_inc(g_zeros, 16)
                    sp.dma_start(agg[h][N:N + P, :], wide[:, 0:W]).then_inc(g_zeros, 16)
                    sp.wait_ge(g_zeros, 32 * (h + 1))
                    sp.sem_inc(g_start, 1)
                    sp.wait_ge(g_free, TILES * (h + 1) + 1)
                sp.dma_start(agg_sb[h], by_node(agg[h][0:N, :])).then_inc(agg_in, 16)
            sp.wait_ge(rows_ready, stores + 1)
            sp.dma_start(by_node(out), xs[:, :, :]).then_inc(out_stored, 16)
            sp.wait_ge(out_stored, 16)

        @block.gpsimd
        def _(pool):
            nc.gpsimd.iota(iota_row[:, :], pattern=[[1, P]], base=0, channel_multiplier=0,
                           allow_small_or_imprecise_dtypes=True).then_inc(consts, 1)
            nc.gpsimd.iota(iota_col[:, :], pattern=[[0, 1]], base=0, channel_multiplier=1,
                           allow_small_or_imprecise_dtypes=True).then_inc(consts, 1)
            nc.gpsimd.iota(spare[:, :], pattern=[[0, 1]], base=N, channel_multiplier=1,
                           allow_small_or_imprecise_dtypes=True).then_inc(consts, 1)
            nc.gpsimd.memset(ones[:, :], 1.0).then_inc(consts, 1)
            nc.gpsimd.memset(summed[:, :, :], 0.0).then_inc(consts, 1)
            nc.gpsimd.memset(carry[:, :, :], 0.0).then_inc(consts, 1)
            nc.gpsimd.memset(idx_src[:, G * K:], 0).then_inc(consts, 1)
            nc.gpsimd.memset(idx_rel[:, G * K:], 0).then_inc(consts, 1)
            pool.sem_inc(group_done, U)
            pool.sem_inc(summed_free, U)
            pool.sem_inc(evacuated, 1)
            pool.sem_inc(g_free, 1)
            pool.sem_inc(proj_free, 1)
            pool.wait_ge(setup, 1)
            ok = pool.value_load(flag[0:1, 0:1], min_val=0, max_val=1)
            for h in range(HOPS):
                pool.wait_ge(table_ready, h + 1)
                with pool.If(ok == 1):
                    with pool.Fori(0, IT) as i:
                        for u in range(U):
                            pool.wait_ge(group_done, i * U + (h * G + u + 1))
                            pool.wait_ge(idx_ready, i * U + (h * (G + U) + u + 1))
                            pool.sem_inc(paced, 1)
                            for k in range(K):
                                pool.indirect_dma_start(
                                    out=rows[:, u, k, 0:D], out_offset=None, in_=table[h],
                                    in_offset=bass.IndirectOffsetOnAxis(ap=idx_now[:, u * K + k:u * K + k + 1], axis=0),
                                ).then_inc(gathered[u], 16)
                with pool.Else():
                    pool.wait_ge(g_start, h + 1)
                    with pool.Fori(0, TILES) as t:
                        pool.wait_ge(g_idx, t + (h * TILES + 1))
                        pool.sem_inc(paced, 1)
                        pool.indirect_dma_start(
                            out=grow[:, 0:D], out_offset=None, in_=table[h],
                            in_offset=bass.IndirectOffsetOnAxis(ap=gidx[:, 0:1], axis=0)).then_inc(g_rows[h], 16)
                        pool.wait_ge(g_merged, t + (h * TILES + 1))
                        pool.sem_inc(paced, 1)
                        pool.indirect_dma_start(
                            out=agg[h], out_offset=bass.IndirectOffsetOnAxis(ap=didx[:, 0:1], axis=0),
                            in_=merged[:, 0:width[h]], in_offset=None, compute_op=ALU.add).then_inc(g_scat[h], 16)
                        pool.wait_ge(g_scat[h], t * 16 + 16)
                        pool.sem_inc(g_free, 1)

        @block.scalar
        def _(act):
            asked = [0]

            def for_vector(make):
                asked[0] += 1
                act.wait_ge(v_out, asked[0])
                make().then_inc(a_out, 1)

            def layernorm():
                for_vector(lambda: nc.scalar.activation(scratch, hs[:, :, :], ACT.Square))
                for_vector(lambda: nc.scalar.activation(st2[:, :], st1[:, :], ACT.Sqrt))

            def transposes(first):
                act.wait_ge(node_ready, 1 if first else 2)
                with act.Fori(0, STEPS) as i:
                    if first:
                        act.wait_ge(turned, i + 1)
                    else:
                        act.wait_ge(turned, i + (STEPS + 1))
                    nc.scalar.copy(stage[:, :, :], hs[:, bass.ds(i * C4, C4), :]).then_inc(staged, 1)

            def load_attr(i):
                act.dma_start(attr[:, :, :], attr_d[bass.ds(i, 1), :, :, :].rearrange("a p u f -> (a p) u f")
                              ).then_inc(attr_in, 16)

            def gates(i):
                act.wait_ge(attr_used, i + 1)
                act.sem_inc(act_paced, 1)
                nc.scalar.activation(w_att[:, bass.ds(i * (U * K), U * K)], z25[:, :], ACT.Sigmoid).then_inc(gate_ready, 1)

            act.wait_ge(setup, 1)
            ok = act.value_load(flag[0:1, 0:1], min_val=0, max_val=1)
            layernorm()
            for h in range(HOPS):
                if h == 4:
                    act.dma_start(attr[:, :, :], attr_d[0, :, :, :]).then_inc(attr_in, 16)
                with act.If(ok == 1):
                    with act.Fori(0, IT) as i:
                        if h == 4:
                            gates(i)
                            load_attr((i + 1) % IT)
                        for u in range(U):
                            act.wait_ge(summed_free, i * U + (h * G + u + 1))
                            act.wait_ge(group_done, i * U + (h * G + u + 1 + U))
                            nc.scalar.copy(summed[:, u, 0:width[h]], acc[u][:, 0:width[h]]).then_inc(evacuated, 1)
                with act.Else():
                    if h == 4:
                        with act.Fori(0, IT) as i:
                            gates(i)
                            load_attr((i + 1) % IT)
                    with act.Fori(0, TILES) as t:
                        act.wait_ge(g_sum, t + (h * TILES + 1))
                        nc.scalar.copy(merged[:, 0:width[h]], bank[1][:, 0:width[h]]).then_inc(g_merged, 1)
                if h == 0:
                    for_vector(lambda: nc.scalar.activation(dinv[:, :], deg[:, :], ACT.Sqrt))
                    layernorm()
                    transposes(True)
                elif h == 1:
                    layernorm()
                elif h == 3:
                    transposes(False)
                    for_vector(lambda: nc.scalar.activation(hs[:, :, :], hs[:, :, :], ACT.Exp))
                    layernorm()
            act.wait_ge(attr_in, 16 * (IT + 1))

        @block.tensor
        def _(pe):
            pe.wait_ge(consts, 8)
            pe.wait_ge(base_f, 1)
            nc.tensor.matmul(bank[0][:, 0:512], ones[0:1, :], base_row[0:1, 0:512], start=True, stop=True)
            nc.tensor.matmul(bank[1][:, 0:G + 1 - 512], ones[0:1, :], base_row[0:1, 512:G + 1],
                             start=True, stop=True).then_inc(base_b, 1)
            pe.wait_ge(ok_col, 1)
            nc.tensor.matmul(bank[2][0:1, 0:1], ones[:, 0:1], mins[:, 3:4], start=True, stop=True).then_inc(ok_sum, 1)
            pe.sem_inc(turned, 1)
            pe.wait_ge(setup, 1)
            ok = pe.value_load(flag[0:1, 0:1], min_val=0, max_val=1)

            def project(first):
                step0 = 0 if first else STEPS
                with pe.Fori(0, STEPS) as i:
                    pe.wait_ge(staged, i + (step0 + 1))
                    pe.sem_inc(pe_paced, 1)
                    for c in range(C4):
                        last = nc.tensor.transpose(bank[5][0:D, c * NP:(c + 1) * NP], stage[:, c, :], ident[0:NP, 0:NP])
                    last.then_inc(turned, 1)
                    pe.wait_ge(h_t_ready, i + (step0 + 1))
                    for c in range(C4):
                        turned_c = h_t[:, c * NP:(c + 1) * NP]
                        if first:
                            pe.wait_ge(banks_free, i * C4 + (c + 1))
                            nc.tensor.matmul(bank[c % 2][0:NP, 0:R * D], turned_c, w_all[:, 0:R * D], start=True, stop=True)
                            nc.tensor.matmul(bank[2 + c % 2][0:NP, 0:D], turned_c, w_all[:, R * D:],
                                             start=True, stop=True).then_inc(projected, 1)
                        else:
                            last = nc.tensor.matmul(bank[0][0:NP, c * D:(c + 1) * D], turned_c, w2_sb[:, :],
                                                    start=True, stop=True)
                    if not first:
                        last.then_inc(projected, 1)

            pe.sem_inc(banks_free, 2)
            for h in range(HOPS):
                W = width[h]
                with pe.If(ok == 1):
                    with pe.Fori(0, IT) as i:
                        for u in range(U):
                            prev = (u - 1) % U
                            pe.wait_ge(pick_ready, i * U + (h * G + u + 1))
                            pe.wait_ge(gathered[u], i * (16 * K) + 16 * K * (h * IT + 1))
                            for k in range(K):
                                nc.tensor.matmul(acc[u][:, 0:W], pick[:, k, :], rows[:, u, k, 0:W],
                                                 start=(k == 0), stop=False)
                            pe.wait_ge(evacuated, i * U + (h * G + u + 1))
                            nc.tensor.matmul(acc[u][:, 0:W], carry[:, u, :], summed[:, prev, 0:W],
                                             start=False, stop=True).then_inc(group_done, 1)
                with pe.Else():
                    with pe.Fori(0, TILES) as t:
                        pe.wait_ge(g_diag, t + (h * TILES + 1))
                        nc.tensor.matmul(bank[0][:, 0:P], ones[:, :], diag[:, :], start=True, stop=True).then_inc(g_dst, 1)
                        pe.wait_ge(g_same, t + (h * TILES + 1))
                        pe.wait_ge(g_rows[h], t * 16 + 16)
                        nc.tensor.matmul(bank[1][:, 0:W], same_w[:, :], grow[:, 0:W], start=True, stop=True
                                         ).then_inc(g_sum, 1)
                if h == 0:
                    project(True)
                if h == 3:
                    project(False)

        @block.vector
        def _(dve):
            made = [0]

            def link(ins):
                made[0] += 1
                ins.then_inc(v, 1)
                dve.wait_ge(v, made[0])

            asked = [0]

            def ask(ins):
                asked[0] += 1
                ins.then_inc(v_out, 1)
                dve.wait_ge(a_out, asked[0])

            def over(ap, shape):
                return ap.to_broadcast(shape)

            NCD = [NP, NC, D]

            def each(ap):
                return ap[:, :].rearrange("p (c o) -> p c o", o=1).to_broadcast(NCD)

            def layernorm():
                link(nc.vector.tensor_reduce(st1[:, :], xs[:, :, :], AX, ALU.add))
                link(nc.vector.tensor_scalar(st2[:, :], st1[:, :], -1.0 / D, None, ALU.mult))
                ask(nc.vector.tensor_tensor(hs[:, :, :], xs[:, :, :], each(st2), ALU.add))
                link(nc.vector.tensor_reduce(st2[:, :], scratch, AX, ALU.add))
                ask(nc.vector.tensor_scalar(st1[:, :], st2[:, :], 1.0 / D, EPS, ALU.mult, ALU.add))
                link(nc.vector.reciprocal(st1[:, :], st2[:, :]))
                return nc.vector.scalar_tensor_tensor(hs[:, :, :], hs[:, :, :], 0.0, each(st1), ALU.max, ALU.mult)

            dve.wait_ge(consts, 8)
            link(nc.vector.tensor_scalar(ident[:, :], iota_row[:, :], iota_col[:, 0:1], None, ALU.is_equal))
            link(nc.vector.tensor_scalar(earlier[:, :], iota_row[:, :], iota_col[:, 0:1], None, ALU.is_lt))
            dve.wait_ge(loaded, 16 * LOADS)
            link(nc.vector.tensor_copy(base_row[0:1, 0:G], base_i[0:1, :]))
            link(nc.vector.memset(base_row[0:1, 0:1], 0.0))
            link(nc.vector.tensor_scalar(base_row[0:1, G:G + 1], base_row[0:1, G - 1:G], float(P - 1), None, ALU.add))
            link(nc.vector.tensor_copy(base_i[0:1, :], base_row[0:1, 0:G]))
            dve.sem_inc(base_f, 1)
            for c in range(2):
                part = slice(c * (G * K // 2), G * K if c else G * K // 2)
                n = part.stop - part.start
                link(nc.vector.tensor_copy(wide[:, 0:n], idx_rel[:, part]))
                link(nc.vector.tensor_copy(wide[:, n:2 * n], idx_src[:, part]))
                link(nc.vector.scalar_tensor_tensor(wide[:, 0:n], wide[:, 0:n], float(N), wide[:, n:2 * n],
                                                    ALU.mult, ALU.add))
                link(nc.vector.tensor_copy(idx_rel[:, part], wide[:, 0:n]))
            dve.wait_ge(base_b, 1)
            nc.vector.tensor_copy(base[:, 0:512], bank[0][:, 0:512])
            link(nc.vector.tensor_copy(base[:, 512:G + 1], bank[1][:, 0:G + 1 - 512]))
            link(nc.vector.tensor_copy(wide[:, 0:G * K], off[:, :].bitcast(i32)))
            wide_g = wide[:, 0:G * K].rearrange("p (g k) -> p g k", k=K)
            link(nc.vector.tensor_tensor(off_g, wide_g, over(base[:, 0:G].rearrange("p (g o) -> p g o", o=1), [P, G, K]),
                                         ALU.subtract))
            link(nc.vector.tensor_tensor(delta[:, :], base[:, 1:G + 1], base[:, 0:G], ALU.subtract))
            nc.vector.memset(carry_at[:, 0:1], -1.0)
            link(nc.vector.tensor_copy(carry_at[:, 1:G], delta[:, 0:G - 1]))
            link(nc.vector.tensor_tensor(wide_g, over(delta[:, :].rearrange("p (g o) -> p g o", o=1), [P, G, K]), off_g,
                                         ALU.subtract))
            link(nc.vector.tensor_reduce(mins[:, 0:1], wide[:, 0:G * K], AX, ALU.min))
            link(nc.vector.tensor_reduce(mins[:, 1:2], off[:, :], AX, ALU.min))
            link(nc.vector.tensor_reduce(mins[:, 2:3], delta[:, :], AX, ALU.max))
            link(nc.vector.tensor_tensor(mins[:, 0:1], mins[:, 0:1], mins[:, 1:2], ALU.min))
            link(nc.vector.tensor_scalar(mins[:, 2:3], mins[:, 2:3], float(P - 1), None, ALU.is_le))
            link(nc.vector.scalar_tensor_tensor(mins[:, 0:1], mins[:, 0:1], 0.0, mins[:, 2:3], ALU.is_ge, ALU.mult))
            link(nc.vector.scalar_tensor_tensor(mins[:, 3:4], base[:, G - 1:G], float(N - P), mins[:, 0:1],
                                                ALU.is_ge, ALU.mult))
            dve.sem_inc(ok_col, 1)
            dve.wait_ge(ok_sum, 1)
            link(nc.vector.tensor_scalar(flag[0:1, 0:1], bank[2][0:1, 0:1], P - 0.5, None, ALU.is_ge))
            dve.sem_inc(setup, 1)
            ok = dve.value_load(flag[0:1, 0:1], min_val=0, max_val=1)
            layernorm().then_inc(rows_ready, 1)

            def products(i):
                dve.wait_ge(attr_in, i * 16 + 16)
                ps = ps_b[:, :].rearrange("p (o f) -> p o f", o=1).to_broadcast([P, U * K, D])
                nc.vector.tensor_tensor(prod[:, :, :], attr[:, :, :].rearrange("p u (k f) -> p (u k) f", f=D), ps,
                                        ALU.mult).then_inc(prod_ready, 1)
                dve.wait_ge(prod_ready, i + 1)
                nc.vector.tensor_reduce(z25[:, :], prod[:, :, :], AX, ALU.add).then_inc(attr_used, 1)
                dve.wait_ge(gate_ready, i + 1)

            def project(first):
                step0 = 0 if first else STEPS
                with dve.Fori(0, STEPS) as i:
                    dve.wait_ge(turned, i + (step0 + 2))
                    nc.vector.tensor_copy(h_t[:, :], bank[5][0:D, 0:C4 * NP]).then_inc(h_t_ready, 1)
                    if first:
                        dve.wait_ge(proj_free, i + 1)
                        bias = hb_b[:, :].rearrange("p (o f) -> p o f", o=1).to_broadcast([NP, R, D])
                        for c in range(C4):
                            dve.wait_ge(projected, i * C4 + (c + 1))
                            last = nc.vector.tensor_tensor(proj_sb[:, :, c, :],
                                                           bank[c % 2][0:NP, 0:R * D].rearrange("p (r f) -> p r f", f=D),
                                                           bias, ALU.add)
                            if c == C4 - 1:
                                last.then_inc(proj_ready, 1)
                            col = xs[:, bass.ds(i * C4 + c, 1), :].rearrange("p c f -> p (c f)")
                            nc.vector.tensor_tensor(col, col, bank[2 + c % 2][0:NP, 0:D], ALU.add).then_inc(banks_free, 1)
                    else:
                        dve.wait_ge(projected, i + (C4 * STEPS + 1))
                        bias = b2_b[:, :].rearrange("p (o f) -> p o f", o=1).to_broadcast([NP, C4, D])
                        z = bank[0][0:NP, 0:C4 * D].rearrange("p (c f) -> p c f", f=D)
                        nc.vector.tensor_tensor(scratch[:, bass.ds(i * C4, C4), :], z, bias, ALU.add).then_inc(z_ready, 1)
                if not first:
                    dve.wait_ge(z_ready, STEPS)

            for h in range(HOPS):
                W = width[h]
                with dve.If(ok == 1):
                    nc.vector.tensor_copy(idx_now[:, :], index[h][:, 0:U * K]).then_inc(idx_ready, U)
                    with dve.Fori(0, IT) as i:
                        if h == 4:
                            products(i)
                        for u in range(U):
                            dve.wait_ge(group_done, i * U + (h * G + u + U))
                            nc.vector.tensor_scalar(carry[:, u, 0:1], iota_col[:, :], carry_at[:, bass.ds(i * U + u, 1)],
                                                    None, ALU.is_equal)
                            if h == 0:
                                nc.vector.tensor_copy(rows[:, u, :, D], w_edge[:, bass.ds(i * (U * K) + u * K, K)])
                            for k in range(K):
                                col = bass.ds(i * (U * K) + (u * K + k), 1)
                                if weights[h] is None:
                                    last = nc.vector.tensor_scalar(pick[:, k, :], iota_row[:, :], off[:, col], None,
                                                                   ALU.is_equal)
                                else:
                                    last = nc.vector.tensor_scalar(pick[:, k, :], iota_row[:, :], off[:, col],
                                                                   weights[h][:, col], ALU.is_equal, ALU.mult)
                            last.then_inc(pick_ready, 1)
                            dve.wait_ge(gathered[u], i * (16 * K) + 16 * K * (h * IT + 1))
                            nc.vector.tensor_copy(idx_now[:, u * K:(u + 1) * K],
                                                  index[h][:, bass.ds(i * (U * K) + (U + u) * K, K)]).then_inc(idx_ready, 1)
                with dve.Else():
                    nc.vector.memset(wide[:, :], 0.0).then_inc(g_zeroed, 1)
                    if h == 4:
                        with dve.Fori(0, IT) as i:
                            products(i)
                    with dve.Fori(0, G) as g:
                        for k in range(K):
                            n = h * TILES + k
                            dve.wait_ge(g_free, g * K + n + 1)
                            col = bass.ds(g * K + k, 1)
                            nc.vector.tensor_copy(gidx[:, :], index[h][:, col]).then_inc(g_idx, 1)
                            if h == 0:
                                nc.vector.tensor_copy(grow[:, D:D + 1], w_edge[:, col])
                            chain = 0

                            def step(ins):
                                nonlocal chain
                                chain += 1
                                ins.then_inc(g_v, 1)
                                dve.wait_ge(g_v, g * (CHAIN * K) + CHAIN * n + chain)

                            step(nc.vector.tensor_tensor(dcol[:, 0:1], off[:, col], base[:, bass.ds(g, 1)], ALU.add))
                            nc.vector.tensor_scalar(diag[:, :], ident[:, :], dcol[:, 0:1], None, ALU.mult).then_inc(g_diag, 1)
                            dve.wait_ge(g_dst, g * K + n + 1)
                            step(nc.vector.tensor_scalar(same[:, :], bank[0][:, 0:P], dcol[:, 0:1], None, ALU.is_equal))
                            w = 1.0 if weights[h] is None else weights[h][:, col]
                            step(nc.vector.tensor_scalar(same_w[:, :], same[:, :], w, None, ALU.mult))
                            step(nc.vector.tensor_tensor(diag[:, :], same[:, :], earlier[:, :], ALU.mult))
                            step(nc.vector.tensor_reduce(dcol[:, 1:2], diag[:, :], AX, ALU.add))
                            step(nc.vector.tensor_scalar(dcol[:, 1:2], dcol[:, 1:2], 0.0, None, ALU.is_equal))
                            step(nc.vector.scalar_tensor_tensor(dcol[:, 1:2], dcol[:, 0:1], spare[:, 0:1], dcol[:, 1:2],
                                                                ALU.subtract, ALU.mult))
                            assert chain == CHAIN
                            nc.vector.tensor_tensor(didx[:, :], dcol[:, 1:2], spare[:, :], ALU.add).then_inc(g_same, 1)

                dve.wait_ge(agg_in, 16 * (h + 1))
                sums = agg_sb[h][:, :, 0:D]
                if h == 0:
                    link(nc.vector.tensor_scalar(deg[:, :], agg_sb[0][:, :, D], 1.0, None, ALU.add))
                    link(nc.vector.tensor_scalar(dinv2[:, :], deg[:, :], 0.0, None, ALU.is_gt))
                    ask(nc.vector.tensor_scalar(deg[:, :], deg[:, :], 1.2e-38, None, ALU.max))
                    link(nc.vector.reciprocal(dinv[:, :], dinv[:, :]))
                    link(nc.vector.tensor_tensor(dinv[:, :], dinv[:, :], dinv2[:, :], ALU.mult))
                    link(nc.vector.tensor_tensor(dinv2[:, :], dinv[:, :], dinv[:, :], ALU.mult))
                    link(nc.vector.tensor_tensor(xs[:, :, :], xs[:, :, :], sums, ALU.add))
                    layernorm().then_inc(node_ready, 1)
                    project(True)
                elif h == 1:
                    link(nc.vector.tensor_tensor(xs[:, :, :], xs[:, :, :], sums, ALU.add))
                    link(layernorm())
                    nc.vector.tensor_tensor(hs[:, :, :], hs[:, :, :], each(dinv), ALU.mult).then_inc(rows_ready, 1)
                elif h == 2:
                    link(nc.vector.tensor_tensor(hs[:, :, :], hs[:, :, :], sums, ALU.add))
                    nc.vector.tensor_tensor(hs[:, :, :], hs[:, :, :], each(dinv2), ALU.mult).then_inc(rows_ready, 1)
                elif h == 3:
                    link(nc.vector.tensor_tensor(hs[:, :, :], hs[:, :, :], sums, ALU.add))
                    nc.vector.tensor_tensor(hs[:, :, :], hs[:, :, :], each(dinv), ALU.mult).then_inc(node_ready, 1)
                    project(False)
                    ask(nc.vector.tensor_scalar(hs[:, :, :], scratch, 0.0, None, ALU.min))
                    link(nc.vector.tensor_scalar(scratch, scratch, 0.0, None, ALU.max))
                    link(nc.vector.scalar_tensor_tensor(scratch, hs[:, :, :], -1.0, scratch, ALU.add, ALU.add))
                    link(nc.vector.tensor_tensor(xs[:, :, :], xs[:, :, :], scratch, ALU.add))
                    link(layernorm())
                    nc.vector.tensor_tensor(hs[:, :, :], hs[:, :, :], each(cj_sb), ALU.mult).then_inc(rows_ready, 1)
                else:
                    link(nc.vector.tensor_tensor(sums, sums, each(ci_sb), ALU.mult))
                    nc.vector.tensor_tensor(xs[:, :, :], xs[:, :, :], sums, ALU.add).then_inc(rows_ready, 1)


_INS = ["x", "src", "dst", "etype", "edge_attr", "edge_w", "att", "cj", "ci",
        "rel_w", "h_bias", "loop_w", "w_t", "b2", "ps_w"]


def kernel(x, src, dst, edge_attr_64, edge_type_8, edge_weight, edge_weight1, node_vec1, node_vec1_n2,
           L1_gnn_weight, L1_gnn_h_bias, L1_gnn_loop_weight, L2_gnn_W, L2_gnn_b, L3_gnn_ps_w):
    import numpy as np
    import concourse.bacc as bacc
    from concourse.bass_utils import run_bass_kernel_spmd

    def by_edge(a):
        return np.ascontiguousarray(np.asarray(a).reshape(G, P, K).transpose(1, 0, 2).reshape(P, G * K))

    arrays = {
        "x": x, "src": by_edge(src), "dst": by_edge(dst), "etype": by_edge(edge_type_8),
        "edge_attr": edge_attr_64, "edge_w": by_edge(edge_weight), "att": by_edge(edge_weight1),
        "cj": node_vec1, "ci": node_vec1_n2, "rel_w": L1_gnn_weight, "h_bias": L1_gnn_h_bias,
        "loop_w": L1_gnn_loop_weight, "w_t": np.asarray(L2_gnn_W).T, "b2": L2_gnn_b, "ps_w": L3_gnn_ps_w,
    }
    arrays = {f"in_{n}": np.ascontiguousarray(arrays[n]) for n in _INS}
    nc = bacc.Bacc("TRN2", target_bir_lowering=False, num_devices=1)
    args = [nc.dram_tensor(n, a.shape, mybir.dt.from_np(a.dtype), kind="ExternalInput").ap() for n, a in arrays.items()]
    out = nc.dram_tensor("out_x", (N, D), mybir.dt.float32, kind="ExternalOutput").ap()
    gnn_kernel(nc, *args, out)
    r = run_bass_kernel_spmd(nc, [arrays], core_ids=[0])
    return r.results[0]["out_x"]
```

```python
import concourse.bass as bass
from concourse import mybir
from contextlib import ExitStack

N = 12500
E = 400000
D = 64
R = 8
P = 128
WIN = 64
K = 5
GE = P * K
G = E // GE
U = 5
IT = G // U
NP = 125
NC = N // NP
C4 = 4
HOPS = 5
FAST = 2
EPS = 1e-5

S = 2 * U
BN = 64
PAIRS = BN // 2
STEP_PAIRS = [6, 6, 6, 6, 8]
ITH = 39
ND = 4900
DP = ND // NC
G0 = G - S * ITH
GROUPS = [G] * FAST + [G - G0] * (HOPS - FAST)
FIRST = [0] * FAST + [G0] * (HOPS - FAST)
BEFORE = [sum(GROUPS[:h]) for h in range(HOPS)]
ALIGN = 16
CH = 20
REC_ROWS = 12480
EN = 200000
FIELDS = 4

assert G * GE == E and IT * U == G and NP * NC == N and NC % C4 == 0
assert sum(STEP_PAIRS) == PAIRS and DP * NC == ND and ND <= BN * (2 * ITH - 1)
assert CH * P >= PAIRS * (2 * ITH + 2) and REC_ROWS * ALIGN + P - ALIGN <= EN


def gnn_kernel(nc, x, src, dst, src_nat, dst_nat, w_nat, etype, edge_attr, edge_w, att, cj, ci,
               rel_w, h_bias, loop_w, w_t, b2, ps_w, out):
    f32 = mybir.dt.float32
    i32 = mybir.dt.int32
    ALU = mybir.AluOpType
    ACT = mybir.ActivationFunctionType
    AX = mybir.AxisListType.X

    table = [nc.dram_tensor(f"table{h}", [R * N if h == 1 else N, D], f32).ap() for h in range(HOPS)]
    width = [D + 2 if h == 0 else D for h in range(HOPS)]
    dense_sum = nc.dram_tensor("dense_sum", [2 * ITH * BN, D], f32).ap()
    rel_d = nc.dram_tensor("rel_d", [P, G * K], i32).ap()
    gate_d = nc.dram_tensor("gate_d", [P, G * K], f32).ap()
    gate_nat = nc.dram_tensor("gate_nat", [E], f32).ap()
    key_nat = nc.dram_tensor("key_nat", [EN], f32).ap()
    row_nat = nc.dram_tensor("row_nat", [EN], f32).ap()
    by_start = nc.dram_tensor("by_start", [REC_ROWS, FIELDS, P], f32).ap()
    start_d = nc.dram_tensor("start_d", [N], f32).ap()
    records = nc.dram_tensor("records", [CH * P // PAIRS, P, FIELDS * PAIRS], f32).ap()
    agg = [nc.dram_tensor(f"agg{h}", [N + P, width[h]], f32).ap() for h in range(HOPS)]

    def by_node_of(ap, p):
        return ap.rearrange("(p c) f -> p c f", p=p)

    def by_node(ap):
        return by_node_of(ap, NP)

    ctx = ExitStack()
    with ctx:
        def sb(name, shape, dt=f32):
            return ctx.enter_context(nc.sbuf_tensor(name, shape, dt))

        def sem(name):
            return ctx.enter_context(nc.semaphore(name))

        xs = sb("xs", [NP, NC, D])
        hs = sb("hs", [NP, NC, D])
        wide = sb("wide", [P, 2 * NC * BN])
        deg = sb("deg", [NP, NC])
        dinv = sb("dinv", [NP, NC])
        dinv2 = sb("dinv2", [NP, NC])
        st1 = sb("st1", [NP, NC])
        st2 = sb("st2", [NP, NC])
        cj_sb = sb("cj_sb", [NP, NC])
        ci_sb = sb("ci_sb", [NP, NC])
        idx_all = sb("idx_all", [P, (G + U) * K], i32)
        off = sb("off", [P, G * K])
        weight = sb("weight", [P, G * K])
        base = sb("base", [P, G + 1])
        delta = sb("delta", [P, G])
        carry_at = sb("carry_at", [P, G])
        base_row = sb("base_row", [1, G + 1])
        base_i = sb("base_i", [1, G], i32)
        idx_now = sb("idx_now", [P, U * K], i32)
        rows = sb("rows", [P, U, K, D + 2])
        pick = sb("pick", [P, K, WIN])
        carry = sb("carry", [WIN, U, WIN])
        summed = sb("summed", [WIN, U, D + 2])
        attr = sb("attr", [P, U, K * D])
        z25 = sb("z25", [P, U * K])
        gate25 = sb("gate25", [P, U * K])
        rec = sb("rec", [P, 2, FIELDS, PAIRS])
        hot = sb("hot", [P, 2, max(STEP_PAIRS), NP + 2 * NC])
        hot_row = hot[:, :, :, 0:NP]
        hot_key = hot[:, :, :, NP:]
        d_t = sb("d_t", [D, BN])
        d_out = sb("d_out", [BN, D])
        ends = sb("ends", [P, 2, CH])
        rec_i = sb("rec_i", [P, CH], i32)
        tmp20 = sb("tmp20", [P, CH])
        rest20 = sb("rest20", [P, CH])
        key0 = sb("key0", [P, CH])
        rec_all = wide[:, 0:CH * FIELDS * P].rearrange("p (j f e) -> p j f e", f=FIELDS, e=P)
        a_blk = [wide[0:NP, b * NC * BN:(b + 1) * NC * BN].rearrange("p (c n) -> p c n", n=BN) for b in range(2)]
        stage = sb("stage", [NP, C4, D])
        h_t = sb("h_t", [D, C4 * NP])
        assert R * C4 * D <= 2 * max(STEP_PAIRS) * (NP + 2 * NC)
        proj_sb = hot[:, :, :, :].rearrange("p a b c -> p (a b c)")[0:NP, 0:R * C4 * D].rearrange(
            "p (r c f) -> p r c f", r=R, c=C4)
        w_all = sb("w_all", [D, (R + 1) * D])
        w2_sb = sb("w2_sb", [D, D])
        hb_b = sb("hb_b", [NP, D])
        b2_b = sb("b2_b", [NP, D])
        ps_b = sb("ps_b", [P, D])
        iota_row = sb("iota_row", [P, 2 * NC])
        iota_nc = sb("iota_nc", [P, NP])
        iota_col = sb("iota_col", [P, 1])
        ident = sb("ident", [P, P])
        earlier = sb("earlier", [P, P])
        later = sb("later", [P, P])
        ones = sb("ones", [P, P])
        spare = sb("spare", [P, 1])
        mins = sb("mins", [P, 4])
        flag = sb("flag", [1, 2], i32)
        gidx = sb("gidx", [P, 1], i32)
        didx = sb("didx", [P, 1], i32)
        dcol = sb("dcol", [P, 2])
        diag = sb("diag", [P, P])
        same = sb("same", [P, P])
        same_w = sb("same_w", [P, P])
        grow = sb("grow", [P, D + 2])
        merged = sb("merged", [P, D + 2])

        bank = [ctx.enter_context(nc.psum_tensor(f"bank{b}", [P, 512], f32)) for b in range(8)]
        acc = bank[0:2]
        build = bank[2:4]
        d_acc = bank[4:6]
        d_back = bank[6]

        agg_sb = [wide[0:NP, 0:NC * width[h]].rearrange("p (c f) -> p c f", f=width[h]) for h in range(HOPS)]
        scratch = wide[0:NP, 0:NC * D].rearrange("p (c f) -> p c f", f=D)
        off_g = off[:, :].rearrange("p (g k) -> p g k", k=K)
        weighted = [False, True, True, True, True]
        attr_d = edge_attr.rearrange("(i u p k) f -> i p u (k f)", u=U, p=P, k=K)

        loaded = sem("loaded")
        consts = sem("consts")
        v = sem("v")
        v_out = sem("v_out")
        a_out = sem("a_out")
        base_f = sem("base_f")
        base_b = sem("base_b")
        ok_col = sem("ok_col")
        ok_sum = sem("ok_sum")
        setup = sem("setup")
        rel_ready = sem("rel_ready")
        nat_ready = sem("nat_ready")
        nat_stored = sem("nat_stored")
        start_stored = sem("start_stored")
        starts_copied = sem("starts_copied")
        edge_in = sem("edge_in")
        row_total = sem("row_total")
        row_base = sem("row_base")
        starts = sem("starts")
        ends_in = sem("ends_in")
        rec_idx = sem("rec_idx")
        rec_in = sem("rec_in")
        rec_key = sem("rec_key")
        rec_turned = sem("rec_turned")
        rec_back = sem("rec_back")
        rec_stored = sem("rec_stored")
        table_out = sem("table_out")
        rows_ready = sem("rows_ready")
        table_ready = sem("table_ready")
        gathered = [sem(f"gathered{u}") for u in range(U)]
        idx_ready = sem("idx_ready")
        paced = sem("paced")
        pick_ready = sem("pick_ready")
        group_done = sem("group_done")
        evacuated = sem("evacuated")
        stored = sem("stored")
        summed_free = sem("summed_free")
        agg_in = sem("agg_in")
        attr_in = sem("attr_in")
        prod_ready = sem("prod_ready")
        attr_used = sem("attr_used")
        gate_ready = sem("gate_ready")
        gate_stored = sem("gate_stored")
        node_ready = sem("node_ready")
        staged = sem("staged")
        turned = sem("turned")
        h_t_ready = sem("h_t_ready")
        projected = sem("projected")
        banks_free = sem("banks_free")
        proj_ready = sem("proj_ready")
        proj_stored = sem("proj_stored")
        proj_free = sem("proj_free")
        z_ready = sem("z_ready")
        out_stored = sem("out_stored")
        rec_load = [sem(f"rec_load{b}") for b in range(2)]
        hot_ready = sem("hot_ready")
        built = sem("built")
        a_there = sem("a_there")
        applied = sem("applied")
        d_t_ready = sem("d_t_ready")
        d_turned = sem("d_turned")
        d_out_ready = sem("d_out_ready")
        d_stored = sem("d_stored")
        d_out_free = sem("d_out_free")

        class General:

            def __init__(self, first):
                self.first = first
                self.zeroed = sem(f"g_zeroed{first}")
                self.zeros = sem(f"g_zeros{first}")
                self.start = sem(f"g_start{first}")
                self.idx = sem(f"g_idx{first}")
                self.diag = sem(f"g_diag{first}")
                self.dst = sem(f"g_dst{first}")
                self.v = sem(f"g_v{first}")
                self.same = sem(f"g_same{first}")
                self.sum = sem(f"g_sum{first}")
                self.merged = sem(f"g_merged{first}")
                self.free = sem(f"g_free{first}")

        g_rows = [sem(f"g_rows{h}") for h in range(HOPS)]
        g_scat = [sem(f"g_scat{h}") for h in range(HOPS)]
        general = [General(0)] * FAST
        general += [General(FAST)] * (HOPS - FAST)

        LOADS = 16
        CONSTS = 12
        STEPS = NC // C4
        TILES = G * K
        CHAIN = 7
        QUADS = PAIRS // 2
        HOP_QUADS = 2 * ITH * QUADS
        BUILT = STEP_PAIRS[-1] // 2 + 1
        SRC_AT, DST_AT, REL_AT = NC * D, NC * D + EN // NP, NC * D + 2 * (EN // NP)
        assert REL_AT + G * K <= 2 * NC * BN

        def slot_rows(h, i, per, n):
            return i * (16 * K * per // U) + 16 * K * (BEFORE[h] // U + n // U + 1)

        block = ctx.enter_context(nc.Block())

        @block.sync
        def _(sp):
            sp.dma_start(xs[:, :, :], by_node(x)).then_inc(loaded, 16)
            for to, of in ((off[:, :].bitcast(i32), dst), (idx_all[:, 0:G * K], src), (weight[:, :], edge_w),
                           (wide[:, REL_AT:REL_AT + G * K].bitcast(i32), etype),
                           (wide[0:NP, SRC_AT:DST_AT].bitcast(i32), src_nat[0:EN].rearrange("(p j) -> p j", p=NP)),
                           (wide[0:NP, DST_AT:REL_AT].bitcast(i32), dst_nat[0:EN].rearrange("(p j) -> p j", p=NP))):
                sp.dma_start(to, of).then_inc(loaded, 16)
            with nc.allow_non_contiguous_dma(reason="625 words, once"):
                sp.dma_start(base_i[0:1, :], dst.rearrange("p (g k) -> p k g", k=K)[0:1, 0, :]).then_inc(loaded, 16)
            sp.dma_start(cj_sb[:, :], cj.rearrange("(p c) o -> p (c o)", p=NP)).then_inc(loaded, 16)
            sp.dma_start(ci_sb[:, :], ci.rearrange("(p c) o -> p (c o)", p=NP)).then_inc(loaded, 16)
            sp.dma_start(w_all[:, 0:R * D].rearrange("i (r o) -> i r o", r=R),
                         rel_w.rearrange("r i o -> i r o")).then_inc(loaded, 16)
            sp.dma_start(w_all[:, R * D:], loop_w).then_inc(loaded, 16)
            sp.dma_start(w2_sb[:, :], w_t).then_inc(loaded, 16)
            sp.dma_start(hb_b[:, :], h_bias.rearrange("(a f) -> a f", a=1).to_broadcast([NP, D])).then_inc(loaded, 16)
            sp.dma_start(b2_b[:, :], b2.rearrange("(a f) -> a f", a=1).to_broadcast([NP, D])).then_inc(loaded, 16)
            sp.dma_start(ps_b[:, :], ps_w.to_broadcast([P, D])).then_inc(loaded, 16)

            def copy_starts(field, nat):
                rows_of = bass.AP(nat.tensor, 0, [[ALIGN, REC_ROWS], [1, P]])
                sp.dma_start(by_start[:, field, :], rows_of).then_inc(starts_copied, 16)

            def store_group(h, i, per, u, slot):
                start = sp.value_load(base_i[0:1, bass.ds(i * per + (FIRST[h] + u), 1)], min_val=0, max_val=N - 1)
                sp.wait_ge(evacuated, i * per + (BEFORE[h] + u + 2))
                sp.dma_start(agg[h][bass.ds(start, WIN), :], summed[:, slot, 0:width[h]]).then_inc(stored, 16)
                sp.wait_ge(stored, i * (16 * per) + 16 * (BEFORE[h] + u + 1))
                sp.sem_inc(summed_free, 1)

            def load_records(m, b):
                to = rec[:, b, :, :].rearrange("p f w -> p (f w)")
                sp.dma_start(to, records[bass.ds(m, 1), :, :].rearrange("a p x -> (a p) x")).then_inc(rec_load[b], 16)

            def general_hop(h):
                q = general[h]
                n = h - q.first
                sp.wait_ge(q.zeroed, n + 1)
                sp.dma_start(agg[h][0:N, :].rearrange("(p c) f -> p (c f)", p=NP),
                             wide[0:NP, 0:NC * width[h]]).then_inc(q.zeros, 16)
                sp.dma_start(agg[h][N:N + P, :], wide[:, 0:width[h]]).then_inc(q.zeros, 16)
                sp.wait_ge(q.zeros, 32 * (n + 1))
                sp.sem_inc(q.start, 1)
                sp.wait_ge(q.free, TILES * (n + 1) + 1)
                sp.dma_start(agg_sb[h], by_node(agg[h][0:N, :])).then_inc(agg_in, 16)
                if h >= FAST:
                    sp.sem_inc(agg_in, 16)

            sp.wait_ge(setup, 1)
            ok = sp.value_load(flag[0:1, 0:1], min_val=0, max_val=1)
            hyb = None
            stores = 0
            for h in range(HOPS):
                if h == 1:
                    t1 = table[1].rearrange("(r p c) f -> p r c f", r=R, p=NP)
                    with sp.Fori(0, STEPS) as i:
                        sp.wait_ge(proj_ready, i + 1)
                        for r in range(R):
                            sp.dma_start(t1[:, r, bass.ds(i * C4, C4), :], proj_sb[:, r, :, :]).then_inc(proj_stored, 16)
                        sp.wait_ge(proj_stored, i * (16 * R) + 16 * R)
                        sp.sem_inc(proj_free, 1)
                else:
                    stores += 1
                    sp.wait_ge(rows_ready, stores)
                    sp.dma_start(by_node(table[h]), hs[:, :, :]).then_inc(table_out, 16)
                    if h == 0:
                        sp.wait_ge(rel_ready, 1)
                        sp.dma_start(rel_d, wide[:, REL_AT:REL_AT + G * K].bitcast(i32)).then_inc(nat_stored, 16)
                        sp.wait_ge(nat_ready, 1)
                        per_p = EN // NP
                        sp.dma_start(row_nat.rearrange("(p j) -> p j", p=NP), wide[0:NP, 3 * per_p:4 * per_p]
                                     ).then_inc(nat_stored, 16)
                        sp.dma_start(key_nat.rearrange("(p j) -> p j", p=NP), wide[0:NP, SRC_AT:DST_AT]
                                     ).then_inc(nat_stored, 16)
                    sp.wait_ge(table_out, 16 * stores)
                sp.sem_inc(table_ready, 1)
                if h == 0:
                    sp.wait_ge(nat_stored, 48)
                    copy_starts(0, key_nat)
                    copy_starts(1, row_nat)
                    copy_starts(2, w_nat)
                if h == FAST:
                    for j in range(CH):
                        sp.wait_ge(rec_back, j + 1)
                        n = P // PAIRS
                        sp.dma_start(records[n * j:n * (j + 1), :, :].rearrange("b p x -> p b x"),
                                     rec_all[:, j, :, :].rearrange("p b x -> p b x")).then_inc(rec_stored, 16)
                    sp.wait_ge(rec_stored, 16 * CH)
                    sp.wait_ge(setup, 2)
                    hyb = sp.value_load(flag[0:1, 1:2], min_val=0, max_val=1)
                if h < FAST:
                    with sp.If(ok == 1):
                        with sp.Fori(0, IT) as i:
                            for u in range(U):
                                store_group(h, i, U, u, u)
                        sp.wait_ge(idx_ready, BEFORE[h] + U * h + GROUPS[h] + U)
                        sp.dma_start(agg_sb[h], by_node(agg[h][0:N, :])).then_inc(agg_in, 16)
                    with sp.Else():
                        general_hop(h)
                else:
                    with sp.If(hyb == 1):
                        hh = h - FAST
                        load_records(0, 0)
                        load_records(1, 1)
                        with sp.Fori(0, ITH) as i:
                            for s in range(S):
                                store_group(h, i, S, s, s % U)
                                if s % U < U - 1:
                                    continue
                                b = s // U
                                sp.wait_ge(d_out_ready, i * 2 + (2 * ITH * hh + b + 1))
                                sp.dma_start(dense_sum[bass.ds(i * (2 * BN) + b * BN, BN), :], d_out[:, :]
                                             ).then_inc(d_stored, 16)
                                sp.wait_ge(hot_ready, i * S + (S * ITH * hh + s + 1))
                                load_records(i * 2 + (b + 2), b)
                                sp.wait_ge(d_stored, i * 32 + 16 * (2 * ITH * hh + b + 1))
                                sp.sem_inc(d_out_free, 1)
                        for b in range(2):
                            sp.wait_ge(rec_load[b], 16 * (ITH + 1) * (hh + 1))
                        sp.wait_ge(a_there, HOP_QUADS * (hh + 1) + 2)
                        sp.wait_ge(idx_ready, BEFORE[h] + U * h + GROUPS[h] + U)
                        sp.dma_start(agg_sb[h][0:DP], by_node_of(dense_sum[BN:BN + ND, :], DP)).then_inc(agg_in, 16)
                        sp.dma_start(agg_sb[h][DP:NP], by_node_of(agg[h][ND:N, :], NP - DP)).then_inc(agg_in, 16)
                    with sp.Else():
                        general_hop(h)
                if h == 0:
                    sp.dma_start(idx_all[:, 0:G * K], rel_d).then_inc(edge_in, 16)
                    sp.dma_start(weight[:, :], att).then_inc(edge_in, 16)
                    sp.wait_ge(gate_stored, 32 * IT)
                    copy_starts(3, gate_nat)
                    sp.wait_ge(starts, 1)
                    sp.dma_start(start_d.rearrange("(p c) -> p c", p=NP), st1[:, :]).then_inc(start_stored, 16)
                    sp.wait_ge(start_stored, 16)
                    with nc.allow_non_contiguous_dma(reason="2560 words each, once"):
                        for t in range(2):
                            sp.dma_start(ends[:, t, :], bass.AP(start_d.tensor, 2 * t, [[2, P], [2 * P, CH]])
                                         ).then_inc(ends_in, 16)
                elif h == 1:
                    sp.dma_start(idx_all[:, 0:G * K], src).then_inc(edge_in, 16)
                    sp.dma_start(weight[:, :], edge_w).then_inc(edge_in, 16)
                elif h == 3:
                    sp.dma_start(weight[:, :], gate_d).then_inc(edge_in, 16)
            sp.wait_ge(rows_ready, stores + 1)
            sp.dma_start(by_node(out), xs[:, :, :]).then_inc(out_stored, 16)
            sp.wait_ge(out_stored, 16)

        @block.gpsimd
        def _(pool):
            for ap, pattern, first, step in ((iota_row, [[1, 2 * NC]], 0, 0), (iota_nc, [[NC, NP]], 0, 0),
                                             (iota_col, [[0, 1]], 0, 1), (spare, [[0, 1]], N, 1),
                                             (key0, [[2 * NC * P, CH]], 0, 2 * NC)):
                nc.gpsimd.iota(ap[:, :], pattern=pattern, base=first, channel_multiplier=step,
                               allow_small_or_imprecise_dtypes=True).then_inc(consts, 1)
            nc.gpsimd.memset(ones[:, :], 1.0).then_inc(consts, 1)
            nc.gpsimd.memset(summed[:, :, :], 0.0).then_inc(consts, 1)
            nc.gpsimd.memset(carry[:, :, :], 0.0).then_inc(consts, 1)
            nc.gpsimd.memset(rows[:, :, :, D + 1:D + 2], 1.0).then_inc(consts, 1)
            nc.gpsimd.memset(grow[:, D + 1:D + 2], 1.0).then_inc(consts, 1)
            nc.gpsimd.memset(idx_all[:, G * K:], 0).then_inc(consts, 1)
            nc.gpsimd.memset(wide[:, REL_AT + G * K:], 0.0).then_inc(consts, 1)
            pool.sem_inc(group_done, U)
            pool.sem_inc(summed_free, U)
            pool.sem_inc(evacuated, 1)
            pool.sem_inc(proj_free, 1)
            pool.sem_inc(general[0].free, 1)
            pool.sem_inc(general[FAST].free, 1)
            pool.wait_ge(setup, 1)
            ok = pool.value_load(flag[0:1, 0:1], min_val=0, max_val=1)

            def gathers(h, i, per, u):
                slot = u % U
                pool.wait_ge(group_done, i * per + (BEFORE[h] + u + 1))
                pool.wait_ge(idx_ready, i * per + (BEFORE[h] + U * h + u + 1))
                pool.sem_inc(paced, 1)
                for k in range(K):
                    pool.indirect_dma_start(
                        out=rows[:, slot, k, 0:D], out_offset=None, in_=table[h],
                        in_offset=bass.IndirectOffsetOnAxis(ap=idx_now[:, slot * K + k:slot * K + k + 1], axis=0),
                    ).then_inc(gathered[slot], 16)

            def general_hop(h):
                q = general[h]
                n = (h - q.first) * TILES
                pool.wait_ge(q.start, h - q.first + 1)
                with pool.Fori(0, TILES) as t:
                    pool.wait_ge(q.idx, t + (n + 1))
                    pool.sem_inc(paced, 1)
                    pool.indirect_dma_start(
                        out=grow[:, 0:D], out_offset=None, in_=table[h],
                        in_offset=bass.IndirectOffsetOnAxis(ap=gidx[:, 0:1], axis=0)).then_inc(g_rows[h], 16)
                    pool.wait_ge(q.merged, t + (n + 1))
                    pool.sem_inc(paced, 1)
                    pool.indirect_dma_start(
                        out=agg[h], out_offset=bass.IndirectOffsetOnAxis(ap=didx[:, 0:1], axis=0),
                        in_=merged[:, 0:width[h]], in_offset=None, compute_op=ALU.add).then_inc(g_scat[h], 16)
                    pool.wait_ge(g_scat[h], t * 16 + 16)
                    pool.sem_inc(q.free, 1)

            hyb = None
            for h in range(HOPS):
                if h == FAST:
                    pool.wait_ge(starts_copied, 16 * FIELDS)
                    pool.wait_ge(rec_idx, 1)
                    table_s = by_start.rearrange("r f e -> r (f e)")
                    for j in range(CH):
                        pool.indirect_dma_start(
                            out=rec_all[:, j, :, :].rearrange("p f e -> p (f e)"), out_offset=None, in_=table_s,
                            in_offset=bass.IndirectOffsetOnAxis(ap=rec_i[:, j:j + 1], axis=0)).then_inc(rec_in, 16)
                    pool.wait_ge(setup, 2)
                    hyb = pool.value_load(flag[0:1, 1:2], min_val=0, max_val=1)
                pool.wait_ge(table_ready, h + 1)
                if h < FAST:
                    with pool.If(ok == 1):
                        with pool.Fori(0, IT) as i:
                            for u in range(U):
                                gathers(h, i, U, u)
                    with pool.Else():
                        general_hop(h)
                else:
                    with pool.If(hyb == 1):
                        with pool.Fori(0, ITH) as i:
                            for s in range(S):
                                gathers(h, i, S, s)
                    with pool.Else():
                        general_hop(h)

        @block.scalar
        def _(act):
            asked = [0]

            def for_vector(make):
                asked[0] += 1
                act.wait_ge(v_out, asked[0])
                make().then_inc(a_out, 1)

            def layernorm():
                for_vector(lambda: nc.scalar.activation(scratch, hs[:, :, :], ACT.Square))
                for_vector(lambda: nc.scalar.activation(st2[:, :], st1[:, :], ACT.Sqrt))

            def stages(first):
                act.wait_ge(node_ready, 1 if first else 2)
                with act.Fori(0, STEPS) as i:
                    act.wait_ge(turned, i + (1 if first else STEPS + 1))
                    nc.scalar.copy(stage[:, :, :], hs[:, bass.ds(i * C4, C4), :]).then_inc(staged, 1)

            def gates(i):
                act.wait_ge(attr_used, i + 1)
                act.sem_inc(paced, 1)
                nc.scalar.activation(gate25[:, :], z25[:, :], ACT.Sigmoid).then_inc(gate_ready, 1)
                act.wait_ge(gate_ready, i + 1)
                act.dma_start(gate_d[:, bass.ds(i * (U * K), U * K)], gate25[:, :]).then_inc(gate_stored, 16)
                act.dma_start(gate_nat.rearrange("(i u p k) -> i p u k", u=U, p=P, k=K)[bass.ds(i, 1), :, :, :]
                              .rearrange("a p u k -> (a p) u k"),
                              gate25[:, :].rearrange("p (u k) -> p u k", u=U)).then_inc(gate_stored, 16)
                act.dma_start(attr[:, :, :], attr_d[bass.ds((i + 1) % IT, 1), :, :, :].rearrange("a p u f -> (a p) u f")
                              ).then_inc(attr_in, 16)

            def evacuate(h, i, per, u):
                act.wait_ge(summed_free, i * per + (BEFORE[h] + u + 1))
                act.wait_ge(group_done, i * per + (BEFORE[h] + u + 1 + U))
                nc.scalar.copy(summed[:, u % U, 0:width[h]], acc[u % 2][0:WIN, 0:width[h]]).then_inc(evacuated, 1)

            def general_hop(h):
                q = general[h]
                with act.Fori(0, TILES) as t:
                    act.wait_ge(q.sum, t + ((h - q.first) * TILES + 1))
                    nc.scalar.copy(merged[:, 0:width[h]], bank[1][:, 0:width[h]]).then_inc(q.merged, 1)

            act.dma_start(attr[:, :, :], attr_d[0, :, :, :]).then_inc(attr_in, 16)
            act.wait_ge(setup, 1)
            ok = act.value_load(flag[0:1, 0:1], min_val=0, max_val=1)
            hyb = None
            layernorm()
            for h in range(HOPS):
                if h == FAST:
                    for j in range(CH):
                        act.wait_ge(rec_turned, j + 1)
                        n = P // PAIRS
                        nc.scalar.copy(
                            rec_all[:, j, :, :].rearrange("p b (f w) -> p b f w", f=FIELDS),
                            bank[j % 2][:, :].rearrange("p (f b w) -> p b f w", f=FIELDS, b=n)).then_inc(rec_back, 1)
                    act.wait_ge(setup, 2)
                    hyb = act.value_load(flag[0:1, 1:2], min_val=0, max_val=1)
                if h < FAST:
                    with act.If(ok == 1):
                        with act.Fori(0, IT) as i:
                            if h == 0:
                                gates(i)
                            for u in range(U):
                                evacuate(h, i, U, u)
                            if h == 0:
                                act.wait_ge(gate_stored, i * 32 + 32)
                    with act.Else():
                        if h == 0:
                            with act.Fori(0, IT) as i:
                                gates(i)
                                act.wait_ge(gate_stored, i * 32 + 32)
                        general_hop(h)
                else:
                    with act.If(hyb == 1):
                        hh = h - FAST
                        with act.Fori(0, ITH) as i:
                            for s in range(S):
                                b, q = s // U, s % U
                                last = q == U - 1
                                first = sum(STEP_PAIRS[:q]) // 2
                                for j in range(first, first + STEP_PAIRS[q] // 2):
                                    act.wait_ge(built, i * (2 * QUADS) + (HOP_QUADS * hh + QUADS * b + j + 1 + BUILT))
                                    nc.scalar.copy(
                                        a_blk[b][:, :, 4 * j:4 * j + 4],
                                        build[j % 2][0:NP, 0:4 * NC].rearrange("p (n c) -> p c n", n=4)).then_inc(a_there, 1)
                                if last:
                                    act.wait_ge(applied, i * 2 + (2 * ITH * hh + b + 1))
                                    nc.scalar.copy(d_t[:, :], d_acc[b][0:D, 0:BN]).then_inc(d_t_ready, 1)
                                evacuate(h, i, S, s)
                                if last:
                                    act.wait_ge(d_out_free, i * 2 + (2 * ITH * hh + b + 1))
                                    act.wait_ge(d_turned, i * 2 + (2 * ITH * hh + b + 1))
                                    nc.scalar.copy(d_out[:, :], d_back[0:BN, 0:D]).then_inc(d_out_ready, 1)
                    with act.Else():
                        general_hop(h)
                if h == 0:
                    for_vector(lambda: nc.scalar.activation(dinv[:, :], deg[:, :], ACT.Sqrt))
                    layernorm()
                    stages(True)
                elif h == 1:
                    layernorm()
                elif h == 3:
                    stages(False)
                    for_vector(lambda: nc.scalar.activation(hs[:, :, :], hs[:, :, :], ACT.Exp))
                    layernorm()
            act.wait_ge(attr_in, 16 * (IT + 1))

        @block.tensor
        def _(pe):
            pe.wait_ge(consts, CONSTS)
            pe.wait_ge(base_f, 1)
            nc.tensor.matmul(bank[0][:, 0:512], ones[0:1, :], base_row[0:1, 0:512], start=True, stop=True)
            nc.tensor.matmul(bank[1][:, 0:G + 1 - 512], ones[0:1, :], base_row[0:1, 512:G + 1],
                             start=True, stop=True).then_inc(base_b, 1)
            pe.wait_ge(ok_col, 1)
            nc.tensor.matmul(bank[2][0:1, 0:1], ones[:, 0:1], mins[:, 3:4], start=True, stop=True).then_inc(ok_sum, 1)
            pe.sem_inc(turned, 1)
            pe.sem_inc(banks_free, 2)
            pe.sem_inc(built, BUILT)
            pe.sem_inc(a_there, 2)
            pe.sem_inc(d_out_free, 1)
            pe.wait_ge(setup, 1)
            ok = pe.value_load(flag[0:1, 0:1], min_val=0, max_val=1)

            def project(first):
                step0 = 0 if first else STEPS
                with pe.Fori(0, STEPS) as i:
                    pe.wait_ge(staged, i + (step0 + 1))
                    pe.sem_inc(paced, 1)
                    for c in range(C4):
                        last = nc.tensor.transpose(bank[7][0:D, c * NP:(c + 1) * NP], stage[:, c, :], ident[0:NP, 0:NP])
                    last.then_inc(turned, 1)
                    pe.wait_ge(h_t_ready, i + (step0 + 1))
                    for c in range(C4):
                        turned_c = h_t[:, c * NP:(c + 1) * NP]
                        if first:
                            pe.wait_ge(banks_free, i * C4 + (c + 1))
                            nc.tensor.matmul(bank[c % 2][0:NP, 0:R * D], turned_c, w_all[:, 0:R * D], start=True, stop=True)
                            nc.tensor.matmul(bank[2 + c % 2][0:NP, 0:D], turned_c, w_all[:, R * D:],
                                             start=True, stop=True).then_inc(projected, 1)
                        else:
                            last = nc.tensor.matmul(bank[0][0:NP, c * D:(c + 1) * D], turned_c, w2_sb[:, :],
                                                    start=True, stop=True)
                    if not first:
                        last.then_inc(projected, 1)

            def sum_group(h, i, per, u):
                W = width[h]
                if u == 0:
                    pe.wait_ge(evacuated, i * per + (BEFORE[h] + u + 1))
                pe.wait_ge(pick_ready, i * per + (BEFORE[h] + u + 1))
                pe.wait_ge(gathered[u % U], slot_rows(h, i, per, u))
                for k in range(K):
                    nc.tensor.matmul(acc[u % 2][0:WIN, 0:W], pick[:, k, :], rows[:, u % U, k, 0:W],
                                     start=(k == 0), stop=False)
                pe.wait_ge(evacuated, i * per + (BEFORE[h] + u + 1))
                pe.sem_inc(paced, 1)
                nc.tensor.matmul(acc[u % 2][0:WIN, 0:W], carry[:, u % U, :], summed[:, (u - 1) % U, 0:W],
                                 start=False, stop=True).then_inc(group_done, 1)

            def general_hop(h):
                q = general[h]
                n = (h - q.first) * TILES
                with pe.Fori(0, TILES) as t:
                    pe.wait_ge(q.diag, t + (n + 1))
                    nc.tensor.matmul(bank[0][:, 0:P], ones[:, :], diag[:, :], start=True, stop=True).then_inc(q.dst, 1)
                    pe.wait_ge(q.same, t + (n + 1))
                    pe.wait_ge(g_rows[h], t * 16 + 16)
                    nc.tensor.matmul(bank[1][:, 0:width[h]], same_w[:, :], grow[:, 0:width[h]], start=True, stop=True
                                     ).then_inc(q.sum, 1)

            hyb = None
            for h in range(HOPS):
                if h == FAST:
                    pe.wait_ge(rec_key, 1)
                    for j in range(CH):
                        if j >= 2:
                            pe.wait_ge(rec_back, j - 1)
                        for f in range(FIELDS):
                            last = nc.tensor.transpose(bank[j % 2][:, f * P:(f + 1) * P], rec_all[:, j, f, :], ident[:, :])
                        last.then_inc(rec_turned, 1)
                    nc.tensor.matmul(bank[2][0:1, 0:1], ones[:, 0:1], mins[:, 3:4], start=True, stop=True
                                     ).then_inc(ok_sum, 1)
                    pe.wait_ge(setup, 2)
                    hyb = pe.value_load(flag[0:1, 1:2], min_val=0, max_val=1)
                if h < FAST:
                    with pe.If(ok == 1):
                        with pe.Fori(0, IT) as i:
                            for u in range(U):
                                sum_group(h, i, U, u)
                    with pe.Else():
                        general_hop(h)
                else:
                    with pe.If(hyb == 1):
                        hh = h - FAST
                        pe.wait_ge(table_ready, h + 1)
                        with pe.Fori(0, ITH) as i:
                            for s in range(S):
                                b, q = s // U, s % U
                                if q == 0:
                                    pe.wait_ge(a_there, i * (2 * QUADS) + (HOP_QUADS * hh + QUADS * b + 2))
                                columns = list(range(q * NC // U, (q + 1) * NC // U))
                                first = sum(STEP_PAIRS[:q]) // 2
                                quads = STEP_PAIRS[q] // 2
                                for j in range(first, first + quads):
                                    part = slice((j - first) * len(columns) // quads, (j - first + 1) * len(columns) // quads)
                                    for c in columns[part]:
                                        last = nc.tensor.matmul(d_acc[b][0:D, 0:BN], hs[:, c, :], a_blk[1 - b][:, c, :],
                                                                start=(c == 0), stop=(c == NC - 1))
                                    if q == U - 1 and j == first + quads - 1:
                                        last.then_inc(applied, 1)
                                    if j == first:
                                        pe.wait_ge(hot_ready, i * S + (S * ITH * hh + s + 1))
                                    pe.wait_ge(a_there, i * (2 * QUADS) + (HOP_QUADS * hh + QUADS * b + j + 1))
                                    for t in range(2):
                                        w = 2 * (j - first) + t
                                        last = nc.tensor.matmul(build[j % 2][0:NP, t * 2 * NC:(t + 1) * 2 * NC],
                                                                hot_row[:, s % 2, w, :], hot_key[:, s % 2, w, :],
                                                                start=True, stop=True)
                                    last.then_inc(built, 1)
                                sum_group(h, i, S, s)
                                if q == U - 1:
                                    pe.wait_ge(d_t_ready, i * 2 + (2 * ITH * hh + b + 1))
                                    pe.sem_inc(paced, 1)
                                    nc.tensor.transpose(d_back[0:BN, 0:D], d_t[:, :], ident[0:D, 0:D]).then_inc(d_turned, 1)
                    with pe.Else():
                        general_hop(h)
                if h == 0:
                    pe.wait_ge(row_total, 1)
                    nc.tensor.matmul(bank[2][0:NP, 0:1], later[0:NP, 0:NP], st2[:, NC - 1:NC], start=True, stop=True
                                     ).then_inc(row_base, 1)
                    project(True)
                if h == 3:
                    project(False)

        @block.vector
        def _(dve):
            made = [0]

            def link(ins):
                made[0] += 1
                ins.then_inc(v, 1)
                dve.wait_ge(v, made[0])

            asked = [0]

            def ask(ins):
                asked[0] += 1
                ins.then_inc(v_out, 1)
                dve.wait_ge(a_out, asked[0])

            def each(ap):
                return ap[:, :].rearrange("p (c o) -> p c o", o=1).to_broadcast([NP, NC, D])

            def each_edge(ap):
                return ap.rearrange("p (g o) -> p g o", o=1).to_broadcast([P, G, K])

            def layernorm():
                link(nc.vector.tensor_reduce(st1[:, :], xs[:, :, :], AX, ALU.add))
                link(nc.vector.tensor_scalar(st2[:, :], st1[:, :], -1.0 / D, None, ALU.mult))
                ask(nc.vector.tensor_tensor(hs[:, :, :], xs[:, :, :], each(st2), ALU.add))
                link(nc.vector.tensor_reduce(st2[:, :], scratch, AX, ALU.add))
                ask(nc.vector.tensor_scalar(st1[:, :], st2[:, :], 1.0 / D, EPS, ALU.mult, ALU.add))
                link(nc.vector.reciprocal(st1[:, :], st2[:, :]))
                return nc.vector.scalar_tensor_tensor(hs[:, :, :], hs[:, :, :], 0.0, each(st1), ALU.max, ALU.mult)

            def floor_div(q, a, d, whole, rest):
                link(nc.vector.tensor_scalar(q, a, 1.0 / d, 0.5 / d - 0.5, ALU.mult, ALU.add))
                link(nc.vector.tensor_copy(whole, q))
                link(nc.vector.tensor_copy(q, whole))
                link(nc.vector.scalar_tensor_tensor(rest, q, -float(d), a, ALU.mult, ALU.add))
                link(nc.vector.tensor_scalar(rest, rest, float(d), None, ALU.is_ge))
                link(nc.vector.tensor_tensor(q, q, rest, ALU.add))

            dve.wait_ge(consts, CONSTS)
            link(nc.vector.tensor_scalar(ident[:, :], iota_row[:, 0:P], iota_col[:, 0:1], None, ALU.is_equal))
            link(nc.vector.tensor_scalar(earlier[:, :], iota_row[:, 0:P], iota_col[:, 0:1], None, ALU.is_lt))
            link(nc.vector.tensor_scalar(later[:, :], iota_row[:, 0:P], iota_col[:, 0:1], None, ALU.is_gt))
            dve.wait_ge(loaded, 16 * LOADS)
            link(nc.vector.tensor_copy(base_row[0:1, 0:G], base_i[0:1, :]))
            link(nc.vector.memset(base_row[0:1, 0:1], 0.0))
            link(nc.vector.tensor_scalar(base_row[0:1, G:G + 1], base_row[0:1, G - 1:G], float(WIN - 1), None, ALU.add))
            link(nc.vector.tensor_copy(base_i[0:1, :], base_row[0:1, 0:G]))
            dve.sem_inc(base_f, 1)
            dve.wait_ge(base_b, 1)
            nc.vector.tensor_copy(base[:, 0:512], bank[0][:, 0:512])
            link(nc.vector.tensor_copy(base[:, 512:G + 1], bank[1][:, 0:G + 1 - 512]))
            link(nc.vector.tensor_copy(wide[:, 0:G * K], off[:, :].bitcast(i32)))
            wide_g = wide[:, 0:G * K].rearrange("p (g k) -> p g k", k=K)
            link(nc.vector.tensor_tensor(off_g, wide_g, each_edge(base[:, 0:G]), ALU.subtract))
            link(nc.vector.tensor_tensor(delta[:, :], base[:, 1:G + 1], base[:, 0:G], ALU.subtract))
            nc.vector.memset(carry_at[:, 0:1], -1.0)
            link(nc.vector.tensor_copy(carry_at[:, 1:G], delta[:, 0:G - 1]))
            link(nc.vector.tensor_tensor(wide_g, each_edge(delta[:, :]), off_g, ALU.subtract))
            link(nc.vector.tensor_reduce(mins[:, 0:1], wide[:, 0:G * K], AX, ALU.min))
            link(nc.vector.tensor_reduce(mins[:, 1:2], off[:, :], AX, ALU.min))
            link(nc.vector.tensor_reduce(mins[:, 2:3], delta[:, :], AX, ALU.max))
            link(nc.vector.tensor_tensor(mins[:, 0:1], mins[:, 0:1], mins[:, 1:2], ALU.min))
            link(nc.vector.tensor_scalar(mins[:, 2:3], mins[:, 2:3], float(WIN - 1), None, ALU.is_le))
            link(nc.vector.scalar_tensor_tensor(mins[:, 0:1], mins[:, 0:1], 0.0, mins[:, 2:3], ALU.is_ge, ALU.mult))
            link(nc.vector.scalar_tensor_tensor(mins[:, 3:4], base[:, G - 1:G], float(N - WIN), mins[:, 0:1],
                                                ALU.is_ge, ALU.mult))
            dve.sem_inc(ok_col, 1)
            dve.wait_ge(ok_sum, 1)
            link(nc.vector.tensor_scalar(flag[0:1, 0:1], bank[2][0:1, 0:1], P - 0.5, None, ALU.is_ge))
            dve.sem_inc(setup, 1)
            ok = dve.value_load(flag[0:1, 0:1], min_val=0, max_val=1)
            layernorm().then_inc(rows_ready, 1)
            types = wide[:, REL_AT:REL_AT + G * K].bitcast(i32)
            link(nc.vector.tensor_copy(wide[:, 0:G * K], types))
            link(nc.vector.tensor_copy(wide[:, G * K:2 * G * K], idx_all[:, 0:G * K]))
            link(nc.vector.scalar_tensor_tensor(wide[:, 0:G * K], wide[:, 0:G * K], float(N), wide[:, G * K:2 * G * K],
                                                ALU.mult, ALU.add))
            link(nc.vector.tensor_copy(types, wide[:, 0:G * K]))
            dve.sem_inc(rel_ready, 1)
            n = EN // NP
            part = [wide[0:NP, t * n:(t + 1) * n] for t in range(4)]
            link(nc.vector.tensor_copy(part[0], wide[0:NP, SRC_AT:DST_AT].bitcast(i32)))
            link(nc.vector.tensor_copy(part[1], wide[0:NP, DST_AT:REL_AT].bitcast(i32)))
            floor_div(part[3], part[0], NC, wide[0:NP, SRC_AT:DST_AT].bitcast(i32), part[2])
            link(nc.vector.tensor_scalar(part[3], part[3], float(NC), None, ALU.mult))
            link(nc.vector.tensor_tensor(part[2], part[0], part[3], ALU.subtract))
            link(nc.vector.scalar_tensor_tensor(wide[0:NP, SRC_AT:DST_AT], part[1], float(NC), part[2],
                                                ALU.mult, ALU.add))
            dve.sem_inc(nat_ready, 1)
            dve.wait_ge(nat_stored, 48)

            def products(i):
                dve.wait_ge(attr_in, i * 16 + 16)
                ps = ps_b[:, :].rearrange("p (o f) -> p o f", o=1).to_broadcast([P, U * K, D])
                features = attr[:, :, :].rearrange("p u (k f) -> p (u k) f", f=D)
                nc.vector.tensor_tensor(features, features, ps, ALU.mult).then_inc(prod_ready, 1)
                dve.wait_ge(prod_ready, i + 1)
                nc.vector.tensor_reduce(z25[:, :], features, AX, ALU.add).then_inc(attr_used, 1)
                dve.wait_ge(gate_ready, i + 1)

            def project(first):
                step0 = 0 if first else STEPS
                with dve.Fori(0, STEPS) as i:
                    dve.wait_ge(turned, i + (step0 + 2))
                    nc.vector.tensor_copy(h_t[:, :], bank[7][0:D, 0:C4 * NP]).then_inc(h_t_ready, 1)
                    if first:
                        dve.wait_ge(proj_free, i + 1)
                        bias = hb_b[:, :].rearrange("p (o f) -> p o f", o=1).to_broadcast([NP, R, D])
                        for c in range(C4):
                            dve.wait_ge(projected, i * C4 + (c + 1))
                            last = nc.vector.tensor_tensor(proj_sb[:, :, c, :],
                                                           bank[c % 2][0:NP, 0:R * D].rearrange("p (r f) -> p r f", f=D),
                                                           bias, ALU.add)
                            if c == C4 - 1:
                                last.then_inc(proj_ready, 1)
                            col = xs[:, bass.ds(i * C4 + c, 1), :].rearrange("p c f -> p (c f)")
                            nc.vector.tensor_tensor(col, col, bank[2 + c % 2][0:NP, 0:D], ALU.add).then_inc(banks_free, 1)
                    else:
                        dve.wait_ge(projected, i + (C4 * STEPS + 1))
                        bias = b2_b[:, :].rearrange("p (o f) -> p o f", o=1).to_broadcast([NP, C4, D])
                        z = bank[0][0:NP, 0:C4 * D].rearrange("p (c f) -> p c f", f=D)
                        nc.vector.tensor_tensor(scratch[:, bass.ds(i * C4, C4), :], z, bias, ALU.add).then_inc(z_ready, 1)
                if not first:
                    dve.wait_ge(z_ready, STEPS)

            def picks(h, i, per, u):
                at = FIRST[h] * K
                dve.wait_ge(group_done, i * per + (BEFORE[h] + u + U))
                nc.vector.tensor_scalar(carry[:, u % U, 0:1], iota_col[0:WIN, :],
                                        carry_at[0:WIN, bass.ds(i * per + (FIRST[h] + u), 1)], None, ALU.is_equal)
                if h == 0:
                    nc.vector.tensor_copy(rows[:, u % U, :, D], weight[:, bass.ds(i * (per * K) + u * K, K)])
                for k in range(K):
                    col = bass.ds(i * (per * K) + (at + u * K + k), 1)
                    if weighted[h]:
                        last = nc.vector.tensor_scalar(pick[:, k, :], iota_row[:, 0:WIN], off[:, col], weight[:, col],
                                                       ALU.is_equal, ALU.mult)
                    else:
                        last = nc.vector.tensor_scalar(pick[:, k, :], iota_row[:, 0:WIN], off[:, col], None,
                                                       ALU.is_equal)
                last.then_inc(pick_ready, 1)
                dve.wait_ge(gathered[u % U], slot_rows(h, i, per, u))
                slot = (u % U) * K
                nc.vector.tensor_copy(idx_now[:, slot:slot + K],
                                      idx_all[:, bass.ds(i * (per * K) + (at + (u + U) * K), K)]).then_inc(idx_ready, 1)

            def first_indices(h):
                at = FIRST[h] * K
                nc.vector.tensor_copy(idx_now[:, :], idx_all[:, at:at + U * K]).then_inc(idx_ready, U)

            def general_hop(h):
                q = general[h]
                nc.vector.memset(wide[:, :], 0.0).then_inc(q.zeroed, 1)
                if h == 0:
                    with dve.Fori(0, IT) as i:
                        products(i)
                with dve.Fori(0, G) as g:
                    for k in range(K):
                        n = (h - q.first) * TILES + k
                        dve.wait_ge(q.free, g * K + n + 1)
                        col = bass.ds(g * K + k, 1)
                        nc.vector.tensor_copy(gidx[:, :], idx_all[:, col]).then_inc(q.idx, 1)
                        if h == 0:
                            nc.vector.tensor_copy(grow[:, D:D + 1], weight[:, col])
                        chain = 0

                        def step(ins):
                            nonlocal chain
                            chain += 1
                            ins.then_inc(q.v, 1)
                            dve.wait_ge(q.v, g * (CHAIN * K) + CHAIN * n + chain)

                        step(nc.vector.tensor_tensor(dcol[:, 0:1], off[:, col], base[:, bass.ds(g, 1)], ALU.add))
                        nc.vector.tensor_scalar(diag[:, :], ident[:, :], dcol[:, 0:1], None, ALU.mult).then_inc(q.diag, 1)
                        dve.wait_ge(q.dst, g * K + n + 1)
                        step(nc.vector.tensor_scalar(same[:, :], bank[0][:, 0:P], dcol[:, 0:1], None, ALU.is_equal))
                        w = weight[:, col] if weighted[h] else 1.0
                        step(nc.vector.tensor_scalar(same_w[:, :], same[:, :], w, None, ALU.mult))
                        step(nc.vector.tensor_tensor(diag[:, :], same[:, :], earlier[:, :], ALU.mult))
                        step(nc.vector.tensor_reduce(dcol[:, 1:2], diag[:, :], AX, ALU.add))
                        step(nc.vector.tensor_scalar(dcol[:, 1:2], dcol[:, 1:2], 0.0, None, ALU.is_equal))
                        step(nc.vector.scalar_tensor_tensor(dcol[:, 1:2], dcol[:, 0:1], spare[:, 0:1], dcol[:, 1:2],
                                                            ALU.subtract, ALU.mult))
                        assert chain == CHAIN
                        nc.vector.tensor_tensor(didx[:, :], dcol[:, 1:2], spare[:, :], ALU.add).then_inc(q.same, 1)

            hyb = None
            loads = agg_loads = 0
            for h in range(HOPS):
                loads += {1: 32, 2: 32, 4: 16}.get(h, 0)
                if loads:
                    dve.wait_ge(edge_in, loads)
                if h < FAST:
                    with dve.If(ok == 1):
                        first_indices(h)
                        with dve.Fori(0, IT) as i:
                            if h == 0:
                                products(i)
                            for u in range(U):
                                picks(h, i, U, u)
                    with dve.Else():
                        general_hop(h)
                else:
                    with dve.If(hyb == 1):
                        hh = h - FAST
                        w_field = 2 if h < 4 else 3
                        first_indices(h)
                        with dve.Fori(0, ITH) as i:
                            for s in range(S):
                                b, q = s // U, s % U
                                if q == 0:
                                    dve.wait_ge(rec_load[b], i * 16 + 16 * ((ITH + 1) * hh + 1))
                                used = QUADS * b + sum(STEP_PAIRS[:q]) // 2 - STEP_PAIRS[q - 1] // 2
                                dve.wait_ge(built, i * (2 * QUADS) + (HOP_QUADS * hh + used + BUILT))
                                first = sum(STEP_PAIRS[:q])
                                for w in range(STEP_PAIRS[q]):
                                    def field(f):
                                        return rec[:, b, f, first + w:first + w + 1]
                                    nc.vector.tensor_scalar(hot_row[:, s % 2, w, :], iota_nc[:, :], field(1), None,
                                                            ALU.is_equal)
                                    last = nc.vector.tensor_scalar(hot_key[:, s % 2, w, :], iota_row[:, :], field(0),
                                                                   field(w_field), ALU.is_equal, ALU.mult)
                                last.then_inc(hot_ready, 1)
                                picks(h, i, S, s)
                    with dve.Else():
                        general_hop(h)

                agg_loads += 16 if h < FAST else 32
                dve.wait_ge(agg_in, agg_loads)
                sums = agg_sb[h][:, :, 0:D]
                if h == 0:
                    link(nc.vector.tensor_scalar(deg[:, :], agg_sb[0][:, :, D], 1.0, None, ALU.add))
                    link(nc.vector.tensor_scalar(dinv2[:, :], deg[:, :], 0.0, None, ALU.is_gt))
                    ask(nc.vector.tensor_scalar(deg[:, :], deg[:, :], 1.2e-38, None, ALU.max))
                    link(nc.vector.reciprocal(dinv[:, :], dinv[:, :]))
                    link(nc.vector.tensor_tensor(dinv[:, :], dinv[:, :], dinv2[:, :], ALU.mult))
                    link(nc.vector.tensor_tensor(dinv2[:, :], dinv[:, :], dinv[:, :], ALU.mult))
                    link(nc.vector.tensor_copy(st1[:, :], agg_sb[0][:, :, D + 1]))
                    nc.vector.memset(deg[:, :], 1.0)
                    link(nc.vector.tensor_tensor(xs[:, :, :], xs[:, :, :], sums, ALU.add))
                    link(nc.vector.tensor_tensor_scan(st2[:, :], deg[:, :], st1[:, :], 0.0, ALU.mult, ALU.add))
                    dve.sem_inc(row_total, 1)
                    link(nc.vector.tensor_tensor(st1[:, :], st2[:, :], st1[:, :], ALU.subtract))
                    dve.wait_ge(row_base, 1)
                    link(nc.vector.tensor_scalar(st1[:, :], st1[:, :], bank[2][0:NP, 0:1], None, ALU.add))
                    dve.sem_inc(starts, 1)
                    dve.wait_ge(start_stored, 16)
                    layernorm().then_inc(node_ready, 1)
                    project(True)
                elif h == 1:
                    link(nc.vector.tensor_tensor(xs[:, :, :], xs[:, :, :], sums, ALU.add))
                    dve.wait_ge(ends_in, 32)
                    floor_div(tmp20[:, :], ends[:, 0, :], ALIGN, rec_i[:, :], rest20[:, :])
                    link(nc.vector.tensor_scalar(rec_i[:, :], tmp20[:, :], float(REC_ROWS - 1), None, ALU.min))
                    link(nc.vector.tensor_tensor(ends[:, 1, :], ends[:, 1, :], ends[:, 0, :], ALU.subtract))
                    link(layernorm())
                    dve.sem_inc(rec_idx, 1)
                    nc.vector.tensor_tensor(hs[:, :, :], hs[:, :, :], each(dinv), ALU.mult).then_inc(rows_ready, 1)
                    dve.wait_ge(rec_in, 16 * CH)
                    keys = rec_all[:, :, 0, :]
                    inside = wide[:, CH * FIELDS * P:CH * (FIELDS + 1) * P].rearrange("p (j e) -> p j e", e=P)
                    key0_b = key0[:, :].rearrange("p (j o) -> p j o", o=1).to_broadcast([P, CH, P])
                    link(nc.vector.tensor_tensor(keys, keys, key0_b, ALU.subtract))
                    link(nc.vector.tensor_scalar(inside, keys, 0.0, None, ALU.is_ge))
                    link(nc.vector.scalar_tensor_tensor(inside, keys, float(2 * NC), inside, ALU.is_lt, ALU.mult))
                    link(nc.vector.tensor_reduce(tmp20[:, :], inside, AX, ALU.add))
                    link(nc.vector.tensor_tensor(tmp20[:, :], tmp20[:, :], ends[:, 1, :], ALU.is_equal))
                    link(nc.vector.tensor_reduce(mins[:, 0:1], tmp20[:, :], AX, ALU.min))
                    link(nc.vector.scalar_tensor_tensor(mins[:, 0:1], base[:, G0:G0 + 1], float(ND), mins[:, 0:1],
                                                        ALU.is_le, ALU.mult))
                    link(nc.vector.tensor_tensor(mins[:, 3:4], mins[:, 3:4], mins[:, 0:1], ALU.mult))
                    dve.sem_inc(rec_key, 1)
                    dve.wait_ge(ok_sum, 2)
                    link(nc.vector.tensor_scalar(flag[0:1, 1:2], bank[2][0:1, 0:1], P - 0.5, None, ALU.is_ge))
                    dve.sem_inc(setup, 1)
                    hyb = dve.value_load(flag[0:1, 1:2], min_val=0, max_val=1)
                    dve.wait_ge(rec_stored, 16 * CH)
                elif h == 2:
                    link(nc.vector.tensor_tensor(hs[:, :, :], hs[:, :, :], sums, ALU.add))
                    nc.vector.tensor_tensor(hs[:, :, :], hs[:, :, :], each(dinv2), ALU.mult).then_inc(rows_ready, 1)
                elif h == 3:
                    link(nc.vector.tensor_tensor(hs[:, :, :], hs[:, :, :], sums, ALU.add))
                    nc.vector.tensor_tensor(hs[:, :, :], hs[:, :, :], each(dinv), ALU.mult).then_inc(node_ready, 1)
                    project(False)
                    ask(nc.vector.tensor_scalar(hs[:, :, :], scratch, 0.0, None, ALU.min))
                    link(nc.vector.tensor_scalar(scratch, scratch, 0.0, None, ALU.max))
                    link(nc.vector.scalar_tensor_tensor(scratch, hs[:, :, :], -1.0, scratch, ALU.add, ALU.add))
                    link(nc.vector.tensor_tensor(xs[:, :, :], xs[:, :, :], scratch, ALU.add))
                    link(layernorm())
                    nc.vector.tensor_tensor(hs[:, :, :], hs[:, :, :], each(cj_sb), ALU.mult).then_inc(rows_ready, 1)
                else:
                    link(nc.vector.tensor_tensor(sums, sums, each(ci_sb), ALU.mult))
                    nc.vector.tensor_tensor(xs[:, :, :], xs[:, :, :], sums, ALU.add).then_inc(rows_ready, 1)


_INS = ["x", "src", "dst", "src_nat", "dst_nat", "w_nat", "etype", "edge_attr", "edge_w", "att", "cj", "ci",
        "rel_w", "h_bias", "loop_w", "w_t", "b2", "ps_w"]


def kernel(x, src, dst, edge_attr_64, edge_type_8, edge_weight, edge_weight1, node_vec1, node_vec1_n2,
           L1_gnn_weight, L1_gnn_h_bias, L1_gnn_loop_weight, L2_gnn_W, L2_gnn_b, L3_gnn_ps_w):
    import numpy as np
    import concourse.bacc as bacc
    from concourse.bass_utils import run_bass_kernel_spmd

    def by_edge(a):
        return np.ascontiguousarray(np.asarray(a).reshape(G, P, K).transpose(1, 0, 2).reshape(P, G * K))

    arrays = {
        "x": x, "src": by_edge(src), "dst": by_edge(dst), "src_nat": src, "dst_nat": dst, "w_nat": edge_weight, "etype": by_edge(edge_type_8),
        "edge_attr": edge_attr_64, "edge_w": by_edge(edge_weight), "att": by_edge(edge_weight1),
        "cj": node_vec1, "ci": node_vec1_n2, "rel_w": L1_gnn_weight, "h_bias": L1_gnn_h_bias,
        "loop_w": L1_gnn_loop_weight, "w_t": np.asarray(L2_gnn_W).T, "b2": L2_gnn_b, "ps_w": L3_gnn_ps_w,
    }
    arrays = {f"in_{n}": np.ascontiguousarray(arrays[n]) for n in _INS}
    nc = bacc.Bacc("TRN2", target_bir_lowering=False, num_devices=1)
    args = [nc.dram_tensor(n, a.shape, mybir.dt.from_np(a.dtype), kind="ExternalInput").ap() for n, a in arrays.items()]
    out = nc.dram_tensor("out_x", (N, D), mybir.dt.float32, kind="ExternalOutput").ap()
    gnn_kernel(nc, *args, out)
    r = run_bass_kernel_spmd(nc, [arrays], core_ids=[0])
    return r.results[0]["out_x"]
```

```python
import concourse.bass as bass
from concourse import mybir
from contextlib import ExitStack

N = 12500
E = 400000
D = 64
R = 8
P = 128
WIN = 64
K = 5
GE = P * K
G = E // GE
U = 5
IT = G // U
NP = 125
NC = N // NP
C4 = 4
HOPS = 5
HYBRID = [0, 2, 3, 4]
EPS = 1e-5

S = 2 * U
BN = 64
PAIRS = BN // 2
STEP_PAIRS = [6, 6, 6, 6, 8]
ITH = 39
ND = 4900
DP = ND // NC
G0 = G - S * ITH
FIRST = [G0 if h in HYBRID else 0 for h in range(HOPS)]
GROUPS = [G - first for first in FIRST]
BEFORE = [sum(GROUPS[:h]) for h in range(HOPS)]
ALIGN = 16
CH = 20
REC_ROWS = 12480
EN = 200000
FIELDS = 4
FIRST_FIELDS = 3

assert G * GE == E and IT * U == G and NP * NC == N and NC % C4 == 0
assert sum(STEP_PAIRS) == PAIRS and DP * NC == ND and ND <= BN * (2 * ITH - 1)
assert CH * P >= PAIRS * (2 * ITH + 2) and REC_ROWS * ALIGN + P - ALIGN <= EN


def gnn_kernel(nc, x, src, dst, src_nat, dst_nat, w_nat, etype, edge_attr, edge_w, att, cj, ci,
               rel_w, h_bias, loop_w, w_t, b2, ps_w, out):
    f32 = mybir.dt.float32
    i32 = mybir.dt.int32
    ALU = mybir.AluOpType
    ACT = mybir.ActivationFunctionType
    AX = mybir.AxisListType.X

    table = [nc.dram_tensor(f"table{h}", [R * N if h == 1 else N, D], f32).ap() for h in range(HOPS)]
    width = [D + 1 if h == 1 else D for h in range(HOPS)]
    dense_sum = nc.dram_tensor("dense_sum", [2 * ITH * BN, D], f32).ap()
    rel_d = nc.dram_tensor("rel_d", [P, G * K], i32).ap()
    gate_d = nc.dram_tensor("gate_d", [P, G * K], f32).ap()
    gate_nat = nc.dram_tensor("gate_nat", [E], f32).ap()
    key_nat = nc.dram_tensor("key_nat", [EN], f32).ap()
    row_nat = nc.dram_tensor("row_nat", [EN], f32).ap()
    by_start = nc.dram_tensor("by_start", [REC_ROWS, FIRST_FIELDS, P], f32).ap()
    by_start_gate = nc.dram_tensor("by_start_gate", [REC_ROWS, P], f32).ap()
    records = nc.dram_tensor("records", [CH * P // PAIRS, P, FIELDS * PAIRS], f32).ap()
    agg = [nc.dram_tensor(f"agg{h}", [N + P, width[h]], f32).ap() for h in range(HOPS)]

    def by_node_of(ap, p):
        return ap.rearrange("(p c) f -> p c f", p=p)

    def by_node(ap):
        return by_node_of(ap, NP)

    ctx = ExitStack()
    with ctx:
        def sb(name, shape, dt=f32):
            return ctx.enter_context(nc.sbuf_tensor(name, shape, dt))

        def sem(name):
            return ctx.enter_context(nc.semaphore(name))

        xs = sb("xs", [NP, NC, D])
        hs = sb("hs", [NP, NC, D])
        wide = sb("wide", [P, 2 * NC * BN])
        deg = sb("deg", [NP, NC])
        dinv = sb("dinv", [NP, NC])
        dinv2 = sb("dinv2", [NP, NC])
        st1 = sb("st1", [NP, NC])
        st2 = sb("st2", [NP, NC])
        cj_sb = sb("cj_sb", [NP, NC])
        ci_sb = sb("ci_sb", [NP, NC])
        idx_all = sb("idx_all", [P, (G + U) * K], i32)
        off = sb("off", [P, G * K])
        weight = sb("weight", [P, G * K])
        base = sb("base", [P, G + 1])
        delta = sb("delta", [P, G])
        carry_at = sb("carry_at", [P, G])
        base_row = sb("base_row", [1, G + 1])
        base_i = sb("base_i", [1, G], i32)
        idx_now = sb("idx_now", [P, U * K], i32)
        rows = sb("rows", [P, U, K, D + 1])
        pick = sb("pick", [P, K, WIN])
        carry = sb("carry", [WIN, U, WIN])
        summed = sb("summed", [WIN, U, D + 1])
        attr = sb("attr", [P, U, K * D])
        z25 = sb("z25", [P, U * K])
        gate25 = sb("gate25", [P, U * K])
        rec = sb("rec", [P, 2, FIELDS, PAIRS])
        hot = sb("hot", [P, 2, max(STEP_PAIRS), NP + 2 * NC])
        hot_row = hot[:, :, :, 0:NP]
        hot_key = hot[:, :, :, NP:]
        d_t = sb("d_t", [D, BN])
        d_out = sb("d_out", [BN, D])
        begins = sb("begins", [P, CH + 1])
        edges = sb("edges", [P, CH])
        node0 = sb("node0", [P, CH])
        rec_i = sb("rec_i", [P, CH], i32)
        tmp20 = sb("tmp20", [P, CH])
        rest20 = sb("rest20", [P, CH])
        key0 = sb("key0", [P, CH])
        rec_all = wide[:, 0:CH * FIRST_FIELDS * P].rearrange("p (j f e) -> p j f e", f=FIRST_FIELDS, e=P)
        GATE_AT = NC * (D + 1)
        rec_gate = wide[:, GATE_AT:GATE_AT + CH * P].rearrange("p (j e) -> p j e", e=P)
        assert CH * GE <= 2 * NC * BN
        dst_of = wide[:, 0:CH * GE]
        a_blk = [wide[0:NP, b * NC * BN:(b + 1) * NC * BN].rearrange("p (c n) -> p c n", n=BN) for b in range(2)]
        stage = sb("stage", [NP, 2, C4, D])
        h_t = sb("h_t", [D, 2, C4 * NP])
        proj_sb = [wide[0:NP, s * R * C4 * D:(s + 1) * R * C4 * D].rearrange("p (r c f) -> p r c f", r=R, c=C4)
                   for s in range(4)]
        w_all = sb("w_all", [D, (R + 1) * D])
        w2_sb = sb("w2_sb", [D, D])
        hb_b = sb("hb_b", [NP, D])
        b2_b = sb("b2_b", [NP, D])
        ps_b = sb("ps_b", [P, D])
        iota_row = sb("iota_row", [P, 2 * NC])
        iota_nc = sb("iota_nc", [P, NP])
        iota_col = sb("iota_col", [P, 1])
        ident = sb("ident", [P, P])
        earlier = sb("earlier", [P, P])
        ones = sb("ones", [P, P])
        spare = sb("spare", [P, 1])
        mins = sb("mins", [P, 4])
        flag = sb("flag", [1, 1], i32)
        gidx = sb("gidx", [P, 1], i32)
        didx = sb("didx", [P, 1], i32)
        dcol = sb("dcol", [P, 2])
        diag = sb("diag", [P, P])
        same = sb("same", [P, P])
        same_w = sb("same_w", [P, P])
        grow = sb("grow", [P, D + 1])
        merged = sb("merged", [P, D + 1])

        bank = [ctx.enter_context(nc.psum_tensor(f"bank{b}", [P, 512], f32)) for b in range(8)]
        acc = bank[0:2]
        build = bank[2:4]
        d_acc = bank[4:6]
        d_back = bank[6]

        agg_sb = [wide[0:NP, 0:NC * width[h]].rearrange("p (c f) -> p c f", f=width[h]) for h in range(HOPS)]
        scratch = wide[0:NP, 0:NC * D].rearrange("p (c f) -> p c f", f=D)
        off_g = off[:, :].rearrange("p (g k) -> p g k", k=K)
        weighted = [False, False, True, True, True]
        attr_d = edge_attr.rearrange("(i u p k) f -> i p u (k f)", u=U, p=P, k=K)

        nat_loaded = sem("nat_loaded")
        loaded = sem("loaded")
        consts = sem("consts")
        v = sem("v")
        v_out = sem("v_out")
        a_out = sem("a_out")
        base_f = sem("base_f")
        base_b = sem("base_b")
        ok_sum = sem("ok_sum")
        setup = sem("setup")
        rel_ready = sem("rel_ready")
        nat_ready = sem("nat_ready")
        nat_stored = sem("nat_stored")
        starts_copied = sem("starts_copied")
        edge_in = sem("edge_in")
        group_idx = sem("group_idx")
        groups_in = sem("groups_in")
        starts = sem("starts")
        ends_in = sem("ends_in")
        rec_idx = sem("rec_idx")
        rec_in = sem("rec_in")
        rec_key = sem("rec_key")
        rec_turned = sem("rec_turned")
        rec_back = sem("rec_back")
        rec_stored = sem("rec_stored")
        gate_copied = sem("gate_copied")
        gate_in = sem("gate_in")
        gate_turned = sem("gate_turned")
        gate_back = sem("gate_back")
        gates_done = sem("gates_done")
        table_out = sem("table_out")
        rows_ready = sem("rows_ready")
        table_ready = sem("table_ready")
        gathered = [sem(f"gathered{u}") for u in range(U)]
        idx_ready = sem("idx_ready")
        paced = sem("paced")
        pick_ready = sem("pick_ready")
        group_done = sem("group_done")
        evacuated = sem("evacuated")
        stored = sem("stored")
        summed_free = sem("summed_free")
        agg_in = sem("agg_in")
        attr_in = sem("attr_in")
        prod_ready = sem("prod_ready")
        scaled = sem("scaled")
        attr_used = sem("attr_used")
        gate_ready = sem("gate_ready")
        gate_stored = sem("gate_stored")
        node_ready = sem("node_ready")
        staged = sem("staged")
        turned = sem("turned")
        h_t_ready = sem("h_t_ready")
        projected = sem("projected")
        banks_free = sem("banks_free")
        proj_ready = sem("proj_ready")
        proj_stored = sem("proj_stored")
        proj_free = sem("proj_free")
        z_ready = sem("z_ready")
        out_stored = sem("out_stored")
        rec_load = [sem(f"rec_load{b}") for b in range(2)]
        hot_ready = sem("hot_ready")
        built = sem("built")
        a_there = sem("a_there")
        applied = sem("applied")
        d_t_ready = sem("d_t_ready")
        d_turned = sem("d_turned")
        d_out_ready = sem("d_out_ready")
        d_stored = sem("d_stored")
        d_out_free = sem("d_out_free")

        class General:

            def __init__(self, first):
                self.first = first
                self.zeroed = sem(f"g_zeroed{first}")
                self.zeros = sem(f"g_zeros{first}")
                self.start = sem(f"g_start{first}")
                self.idx = sem(f"g_idx{first}")
                self.diag = sem(f"g_diag{first}")
                self.dst = sem(f"g_dst{first}")
                self.v = sem(f"g_v{first}")
                self.same = sem(f"g_same{first}")
                self.sum = sem(f"g_sum{first}")
                self.merged = sem(f"g_merged{first}")
                self.free = sem(f"g_free{first}")

        g_rows = [sem(f"g_rows{h}") for h in range(HOPS)]
        g_scat = [sem(f"g_scat{h}") for h in range(HOPS)]
        general = [General(0)] * 2
        general += [General(2)] * (HOPS - 2)

        LOADS = 14
        CONSTS = 11
        STEPS = NC // C4
        assert STEPS % 4 == 1
        TILES = G * K
        CHAIN = 7
        QUADS = PAIRS // 2
        HOP_QUADS = 2 * ITH * QUADS
        BUILT = STEP_PAIRS[-1] // 2 + 1
        SRC_AT, DST_AT, REL_AT = NC * D, NC * D + EN // NP, NC * D + 2 * (EN // NP)
        assert REL_AT + G * K <= 2 * NC * BN

        gcn_w = wide[:, REL_AT:REL_AT + G * K]
        assert GATE_AT + CH * P <= REL_AT

        def overlapping(nat):
            return bass.AP(nat.tensor, 0, [[ALIGN, REC_ROWS], [1, P]])

        def rec_back_at(j):
            n = FIRST_FIELDS * P
            return wide[:, j * n:(j + 1) * n].rearrange("p (b f w) -> p b f w", f=FIRST_FIELDS, w=PAIRS)

        def slot_rows(h, i, per, n):
            return i * (16 * K * per // U) + 16 * K * (BEFORE[h] // U + n // U + 1)

        block = ctx.enter_context(nc.Block())

        @block.sync
        def _(sp):
            for at, of in ((SRC_AT, src_nat), (DST_AT, dst_nat)):
                sp.dma_start(wide[0:NP, at:at + EN // NP].bitcast(i32), of[0:EN].rearrange("(p j) -> p j", p=NP)
                             ).then_inc(nat_loaded, 16)
            sp.dma_start(xs[:, :, :], by_node(x)).then_inc(loaded, 16)
            for to, of in ((off[:, :].bitcast(i32), dst), (idx_all[:, 0:G * K], src), (weight[:, :], att),
                           (wide[:, REL_AT:REL_AT + G * K].bitcast(i32), etype)):
                sp.dma_start(to, of).then_inc(loaded, 16)
            with nc.allow_non_contiguous_dma(reason="625 words, once"):
                sp.dma_start(base_i[0:1, :], dst.rearrange("p (g k) -> p k g", k=K)[0:1, 0, :]).then_inc(loaded, 16)
            sp.dma_start(cj_sb[:, :], cj.rearrange("(p c) o -> p (c o)", p=NP)).then_inc(loaded, 16)
            sp.dma_start(ci_sb[:, :], ci.rearrange("(p c) o -> p (c o)", p=NP)).then_inc(loaded, 16)
            sp.dma_start(w_all[:, 0:R * D].rearrange("i (r o) -> i r o", r=R),
                         rel_w.rearrange("r i o -> i r o")).then_inc(loaded, 16)
            sp.dma_start(w_all[:, R * D:], loop_w).then_inc(loaded, 16)
            sp.dma_start(w2_sb[:, :], w_t).then_inc(loaded, 16)
            sp.dma_start(hb_b[:, :], h_bias.rearrange("(a f) -> a f", a=1).to_broadcast([NP, D])).then_inc(loaded, 16)
            sp.dma_start(b2_b[:, :], b2.rearrange("(a f) -> a f", a=1).to_broadcast([NP, D])).then_inc(loaded, 16)
            sp.dma_start(ps_b[:, :], ps_w.to_broadcast([P, D])).then_inc(loaded, 16)

            def store_group(h, i, per, u, slot):
                start = sp.value_load(base_i[0:1, bass.ds(i * per + (FIRST[h] + u), 1)], min_val=0, max_val=N - 1)
                sp.wait_ge(evacuated, i * per + (BEFORE[h] + u + 2))
                sp.dma_start(agg[h][bass.ds(start, WIN), :], summed[:, slot, 0:width[h]]).then_inc(stored, 16)
                sp.wait_ge(stored, i * (16 * per) + 16 * (BEFORE[h] + u + 1))
                sp.sem_inc(summed_free, 1)

            def load_records(h, m, b):
                n = FIELDS if h == 4 else FIRST_FIELDS
                to = rec[:, b, 0:n, :].rearrange("p f w -> p (f w)")
                sp.dma_start(to, records[bass.ds(m, 1), :, 0:n * PAIRS].rearrange("a p x -> (a p) x")
                             ).then_inc(rec_load[b], 16)

            def general_hop(h):
                q = general[h]
                n = h - q.first
                sp.wait_ge(q.zeroed, n + 1)
                sp.dma_start(agg[h][0:N, :].rearrange("(p c) f -> p (c f)", p=NP),
                             wide[0:NP, 0:NC * width[h]]).then_inc(q.zeros, 16)
                sp.dma_start(agg[h][N:N + P, :], wide[:, 0:width[h]]).then_inc(q.zeros, 16)
                sp.wait_ge(q.zeros, 32 * (n + 1))
                sp.sem_inc(q.start, 1)
                sp.wait_ge(q.free, TILES * (n + 1) + 1)
                sp.dma_start(agg_sb[h], by_node(agg[h][0:N, :])).then_inc(agg_in, 16)
                if h in HYBRID:
                    sp.sem_inc(agg_in, 16)

            sp.wait_ge(nat_ready, 1)
            per_p = EN // NP
            sp.dma_start(row_nat.rearrange("(p j) -> p j", p=NP), wide[0:NP, 3 * per_p:4 * per_p]).then_inc(nat_stored, 16)
            sp.dma_start(key_nat.rearrange("(p j) -> p j", p=NP), wide[0:NP, SRC_AT:DST_AT]).then_inc(nat_stored, 16)
            fast = None
            stores = 0
            for h in range(HOPS):
                if h == 1:
                    t1 = table[1].rearrange("(r p c) f -> p r c f", r=R, p=NP)

                    def store_step(i, s):
                        sp.wait_ge(proj_ready, i * 4 + (s + 1))
                        for r in range(R):
                            sp.dma_start(t1[:, r, bass.ds(i * (4 * C4) + s * C4, C4), :], proj_sb[s][:, r, :, :]
                                         ).then_inc(proj_stored, 16)
                        sp.wait_ge(proj_stored, i * (64 * R) + 16 * R * (s + 1))
                        sp.sem_inc(proj_free, 1)

                    with sp.Fori(0, STEPS // 4) as i:
                        for s in range(4):
                            store_step(i, s)
                    store_step(STEPS // 4, 0)
                else:
                    stores += 1
                    sp.wait_ge(rows_ready, stores)
                    sp.dma_start(by_node(table[h]), hs[:, :, :]).then_inc(table_out, 16)
                    if h == 0:
                        sp.wait_ge(rel_ready, 1)
                        sp.dma_start(rel_d, wide[:, REL_AT:REL_AT + G * K].bitcast(i32)).then_inc(nat_stored, 16)
                    sp.wait_ge(table_out, 16 * stores)
                sp.sem_inc(table_ready, 1)
                if h == 0:
                    for j in range(CH):
                        sp.wait_ge(rec_back, j + 1)
                        n = P // PAIRS
                        sp.dma_start(records[n * j:n * (j + 1), :, 0:FIRST_FIELDS * PAIRS].rearrange("b p x -> p b x"),
                                     rec_back_at(j).rearrange("p b f w -> p b (f w)")).then_inc(rec_stored, 16)
                    sp.wait_ge(rec_stored, 16 * CH)
                    sp.wait_ge(setup, 1)
                    fast = sp.value_load(flag[0:1, 0:1], min_val=0, max_val=1)
                if h == 2:
                    for j in range(CH // 4):
                        sp.wait_ge(gate_back, j + 1)
                        n = 4 * P // PAIRS
                        sp.dma_start(records[n * j:n * (j + 1), :, FIRST_FIELDS * PAIRS:].rearrange("b p w -> p b w"),
                                     rec_gate[:, 4 * j:4 * j + 4, :].rearrange("p j (b w) -> p (j b) w", w=PAIRS)
                                     ).then_inc(rec_stored, 16)
                    sp.wait_ge(rec_stored, 16 * (CH + CH // 4))
                    sp.sem_inc(gates_done, 1)
                if h not in HYBRID:
                    with sp.If(fast == 1):
                        with sp.Fori(0, IT) as i:
                            for u in range(U):
                                store_group(h, i, U, u, u)
                        sp.wait_ge(idx_ready, BEFORE[h] + U * h + GROUPS[h] + U)
                        sp.dma_start(agg_sb[h], by_node(agg[h][0:N, :])).then_inc(agg_in, 16)
                    with sp.Else():
                        general_hop(h)
                else:
                    with sp.If(fast == 1):
                        hh = HYBRID.index(h)
                        load_records(h, 0, 0)
                        load_records(h, 1, 1)
                        with sp.Fori(0, ITH) as i:
                            for s in range(S):
                                store_group(h, i, S, s, s % U)
                                if s % U < U - 1:
                                    continue
                                b = s // U
                                sp.wait_ge(d_out_ready, i * 2 + (2 * ITH * hh + b + 1))
                                sp.dma_start(dense_sum[bass.ds(i * (2 * BN) + b * BN, BN), :], d_out[:, :]
                                             ).then_inc(d_stored, 16)
                                sp.wait_ge(hot_ready, i * S + (S * ITH * hh + s + 1))
                                load_records(h, i * 2 + (b + 2), b)
                                sp.wait_ge(d_stored, i * 32 + 16 * (2 * ITH * hh + b + 1))
                                sp.sem_inc(d_out_free, 1)
                        for b in range(2):
                            sp.wait_ge(rec_load[b], 16 * (ITH + 1) * (hh + 1))
                        sp.wait_ge(a_there, HOP_QUADS * (hh + 1) + 2)
                        sp.wait_ge(idx_ready, BEFORE[h] + U * h + GROUPS[h] + U)
                        sp.dma_start(agg_sb[h][0:DP], by_node_of(dense_sum[BN:BN + ND, :], DP)).then_inc(agg_in, 16)
                        sp.dma_start(agg_sb[h][DP:NP], by_node_of(agg[h][ND:N, :], NP - DP)).then_inc(agg_in, 16)
                    with sp.Else():
                        general_hop(h)
                if h == 0:
                    sp.dma_start(idx_all[:, 0:G * K], rel_d).then_inc(edge_in, 16)
                    sp.dma_start(gcn_w, edge_w).then_inc(edge_in, 16)
                elif h == 1:
                    sp.dma_start(idx_all[:, 0:G * K], src).then_inc(edge_in, 16)
                    sp.dma_start(weight[:, :], edge_w).then_inc(edge_in, 16)
                    sp.wait_ge(gate_stored, 32 * IT)
                    sp.dma_start(by_start_gate, overlapping(gate_nat)).then_inc(gate_copied, 16)
                elif h == 3:
                    sp.dma_start(weight[:, :], gate_d).then_inc(edge_in, 16)
            sp.wait_ge(rows_ready, stores + 1)
            sp.dma_start(by_node(out), xs[:, :, :]).then_inc(out_stored, 16)
            sp.wait_ge(out_stored, 16)

        @block.gpsimd
        def _(pool):
            for ap, pattern, first, step in ((iota_row, [[1, 2 * NC]], 0, 0), (iota_nc, [[NC, NP]], 0, 0),
                                             (iota_col, [[0, 1]], 0, 1), (spare, [[0, 1]], N, 1),
                                             (key0, [[2 * NC * P, CH]], 0, 2 * NC),
                                             (node0, [[2 * P, CH]], 0, 2)):
                nc.gpsimd.iota(ap[:, :], pattern=pattern, base=first, channel_multiplier=step,
                               allow_small_or_imprecise_dtypes=True).then_inc(consts, 1)
            nc.gpsimd.memset(ones[:, :], 1.0).then_inc(consts, 1)
            nc.gpsimd.memset(summed[:, :, :], 0.0).then_inc(consts, 1)
            nc.gpsimd.memset(carry[:, :, :], 0.0).then_inc(consts, 1)
            nc.gpsimd.memset(idx_all[:, G * K:], 0).then_inc(consts, 1)
            nc.gpsimd.memset(wide[:, REL_AT + G * K:], 0.0).then_inc(consts, 1)
            pool.sem_inc(group_done, U)
            pool.sem_inc(summed_free, U)
            pool.sem_inc(evacuated, 1)
            pool.sem_inc(proj_free, 4)
            pool.sem_inc(general[0].free, 1)
            pool.sem_inc(general[2].free, 1)

            def by_chunk(rows_of, to, done):
                for j in range(CH):
                    pool.indirect_dma_start(
                        out=to(j), out_offset=None, in_=rows_of,
                        in_offset=bass.IndirectOffsetOnAxis(ap=rec_i[:, j:j + 1], axis=0)).then_inc(done, 16)

            def gathers(h, i, per, u):
                slot = u % U
                pool.wait_ge(group_done, i * per + (BEFORE[h] + u + 1))
                pool.wait_ge(idx_ready, i * per + (BEFORE[h] + U * h + u + 1))
                pool.sem_inc(paced, 1)
                for k in range(K):
                    pool.indirect_dma_start(
                        out=rows[:, slot, k, 0:D], out_offset=None, in_=table[h],
                        in_offset=bass.IndirectOffsetOnAxis(ap=idx_now[:, slot * K + k:slot * K + k + 1], axis=0),
                    ).then_inc(gathered[slot], 16)

            def general_hop(h):
                q = general[h]
                n = (h - q.first) * TILES
                pool.wait_ge(q.start, h - q.first + 1)
                with pool.Fori(0, TILES) as t:
                    pool.wait_ge(q.idx, t + (n + 1))
                    pool.sem_inc(paced, 1)
                    pool.indirect_dma_start(
                        out=grow[:, 0:D], out_offset=None, in_=table[h],
                        in_offset=bass.IndirectOffsetOnAxis(ap=gidx[:, 0:1], axis=0)).then_inc(g_rows[h], 16)
                    pool.wait_ge(q.merged, t + (n + 1))
                    pool.sem_inc(paced, 1)
                    pool.indirect_dma_start(
                        out=agg[h], out_offset=bass.IndirectOffsetOnAxis(ap=didx[:, 0:1], axis=0),
                        in_=merged[:, 0:width[h]], in_offset=None, compute_op=ALU.add).then_inc(g_scat[h], 16)
                    pool.wait_ge(g_scat[h], t * 16 + 16)
                    pool.sem_inc(q.free, 1)

            pool.wait_ge(group_idx, 1)
            by_chunk(dst_nat.rearrange("(g e) -> g e", e=GE), lambda j: dst_of.bitcast(i32)[:, j * GE:(j + 1) * GE],
                     groups_in)
            pool.wait_ge(starts_copied, 16 * FIRST_FIELDS)
            pool.wait_ge(rec_idx, 1)
            by_chunk(by_start.rearrange("r f e -> r (f e)"), lambda j: rec_all[:, j, :, :].rearrange("p f e -> p (f e)"),
                     rec_in)
            pool.wait_ge(setup, 1)
            fast = pool.value_load(flag[0:1, 0:1], min_val=0, max_val=1)
            for h in range(HOPS):
                if h == 2:
                    pool.wait_ge(gate_copied, 16)
                    by_chunk(by_start_gate, lambda j: rec_gate[:, j, :], gate_in)
                pool.wait_ge(table_ready, h + 1)
                if h not in HYBRID:
                    with pool.If(fast == 1):
                        with pool.Fori(0, IT) as i:
                            for u in range(U):
                                gathers(h, i, U, u)
                    with pool.Else():
                        general_hop(h)
                else:
                    with pool.If(fast == 1):
                        with pool.Fori(0, ITH) as i:
                            for s in range(S):
                                gathers(h, i, S, s)
                    with pool.Else():
                        general_hop(h)

        @block.scalar
        def _(act):
            asked = [0]

            def for_vector(make):
                asked[0] += 1
                act.wait_ge(v_out, asked[0])
                make().then_inc(a_out, 1)

            def layernorm():
                for_vector(lambda: nc.scalar.activation(scratch, hs[:, :, :], ACT.Square))
                for_vector(lambda: nc.scalar.activation(st2[:, :], st1[:, :], ACT.Sqrt))

            def stages(first):
                act.wait_ge(node_ready, 1 if first else 2)
                step0 = 0 if first else STEPS

                def fill(i, s):
                    act.wait_ge(turned, i * 4 + (s + step0 + 1))
                    nc.scalar.copy(stage[:, s % 2, :, :], hs[:, bass.ds(i * (4 * C4) + s * C4, C4), :]).then_inc(staged, 1)

                with act.Fori(0, STEPS // 4) as i:
                    for s in range(4):
                        fill(i, s)
                fill(STEPS // 4, 0)

            def gates(i):
                act.wait_ge(attr_used, i + 1)
                act.sem_inc(paced, 1)
                nc.scalar.activation(gate25[:, :], z25[:, :], ACT.Sigmoid).then_inc(gate_ready, 1)
                act.wait_ge(gate_ready, i + 1)
                act.dma_start(gate_d[:, bass.ds(i * (U * K), U * K)], gate25[:, :]).then_inc(gate_stored, 16)
                act.dma_start(gate_nat.rearrange("(i u p k) -> i p u k", u=U, p=P, k=K)[bass.ds(i, 1), :, :, :]
                              .rearrange("a p u k -> (a p) u k"),
                              gate25[:, :].rearrange("p (u k) -> p u k", u=U)).then_inc(gate_stored, 16)
                act.dma_start(attr[:, :, :], attr_d[bass.ds((i + 1) % IT, 1), :, :, :].rearrange("a p u f -> (a p) u f")
                              ).then_inc(attr_in, 16)

            def evacuate(h, i, per, u):
                act.wait_ge(summed_free, i * per + (BEFORE[h] + u + 1))
                act.wait_ge(group_done, i * per + (BEFORE[h] + u + 1 + U))
                nc.scalar.copy(summed[:, u % U, 0:width[h]], acc[u % 2][0:WIN, 0:width[h]]).then_inc(evacuated, 1)

            def general_hop(h):
                q = general[h]
                with act.Fori(0, TILES) as t:
                    act.wait_ge(q.sum, t + ((h - q.first) * TILES + 1))
                    nc.scalar.copy(merged[:, 0:width[h]], bank[1][:, 0:width[h]]).then_inc(q.merged, 1)

            act.dma_start(attr[:, :, :], attr_d[0, :, :, :]).then_inc(attr_in, 16)
            act.wait_ge(nat_stored, 32)
            for field, nat in enumerate((key_nat, row_nat, w_nat)):
                act.dma_start(by_start[:, field, :], overlapping(nat)).then_inc(starts_copied, 16)
            layernorm()
            fast = None
            for h in range(HOPS):
                if h == 0:
                    for j in range(CH):
                        act.wait_ge(rec_turned, j + 1)
                        nc.scalar.copy(rec_back_at(j), bank[j % 2][:, 0:FIRST_FIELDS * P].rearrange(
                            "p (f b w) -> p b f w", f=FIRST_FIELDS, w=PAIRS)).then_inc(rec_back, 1)
                    act.wait_ge(setup, 1)
                    fast = act.value_load(flag[0:1, 0:1], min_val=0, max_val=1)
                if h == 2:
                    for j in range(CH // 4):
                        act.wait_ge(gate_turned, j + 1)
                        nc.scalar.copy(rec_gate[:, 4 * j:4 * j + 4, :].rearrange("p j e -> p (j e)"), bank[j % 2][:, :]
                                       ).then_inc(gate_back, 1)
                    act.wait_ge(gates_done, 1)
                if h not in HYBRID:
                    with act.If(fast == 1):
                        with act.Fori(0, IT) as i:
                            gates(i)
                            for u in range(U):
                                evacuate(h, i, U, u)
                            act.wait_ge(gate_stored, i * 32 + 32)
                    with act.Else():
                        with act.Fori(0, IT) as i:
                            gates(i)
                            act.wait_ge(gate_stored, i * 32 + 32)
                        general_hop(h)
                else:
                    with act.If(fast == 1):
                        hh = HYBRID.index(h)
                        with act.Fori(0, ITH) as i:
                            for s in range(S):
                                b, q = s // U, s % U
                                last = q == U - 1
                                first = sum(STEP_PAIRS[:q]) // 2
                                for j in range(first, first + STEP_PAIRS[q] // 2):
                                    act.wait_ge(built, i * (2 * QUADS) + (HOP_QUADS * hh + QUADS * b + j + 1 + BUILT))
                                    nc.scalar.copy(
                                        a_blk[b][:, :, 4 * j:4 * j + 4],
                                        build[j % 2][0:NP, 0:4 * NC].rearrange("p (n c) -> p c n", n=4)).then_inc(a_there, 1)
                                if last:
                                    act.wait_ge(applied, i * 2 + (2 * ITH * hh + b + 1))
                                    nc.scalar.copy(d_t[:, :], d_acc[b][0:D, 0:BN]).then_inc(d_t_ready, 1)
                                evacuate(h, i, S, s)
                                if last:
                                    act.wait_ge(d_out_free, i * 2 + (2 * ITH * hh + b + 1))
                                    act.wait_ge(d_turned, i * 2 + (2 * ITH * hh + b + 1))
                                    nc.scalar.copy(d_out[:, :], d_back[0:BN, 0:D]).then_inc(d_out_ready, 1)
                    with act.Else():
                        general_hop(h)
                if h == 0:
                    layernorm()
                    stages(True)
                elif h == 1:
                    for_vector(lambda: nc.scalar.activation(dinv[:, :], deg[:, :], ACT.Sqrt))
                    layernorm()
                elif h == 3:
                    stages(False)
                    for_vector(lambda: nc.scalar.activation(hs[:, :, :], hs[:, :, :], ACT.Exp))
                    layernorm()
            act.wait_ge(attr_in, 16 * (IT + 1))

        @block.tensor
        def _(pe):
            pe.wait_ge(consts, CONSTS)
            pe.wait_ge(base_f, 1)
            nc.tensor.matmul(bank[0][:, 0:512], ones[0:1, :], base_row[0:1, 0:512], start=True, stop=True)
            nc.tensor.matmul(bank[1][:, 0:G + 1 - 512], ones[0:1, :], base_row[0:1, 512:G + 1],
                             start=True, stop=True).then_inc(base_b, 1)
            pe.wait_ge(starts, 1)
            nc.tensor.matmul(bank[2][:, 0:CH], same[:, :], begins[:, 0:CH], start=True, stop=False)
            nc.tensor.matmul(bank[2][:, 0:CH], diag[:, :], begins[:, 1:CH + 1], start=False, stop=True
                             ).then_inc(ends_in, 1)
            pe.sem_inc(turned, 2)
            pe.sem_inc(banks_free, 2)
            pe.sem_inc(built, BUILT)
            pe.sem_inc(a_there, 2)
            pe.sem_inc(d_out_free, 1)

            def project(first):
                step0 = 0 if first else STEPS

                def turn(i, s):
                    pe.wait_ge(staged, i * 4 + (s + step0 + 1))
                    pe.sem_inc(paced, 1)
                    for c in range(C4):
                        last = nc.tensor.transpose(bank[6 + s % 2][0:D, c * NP:(c + 1) * NP], stage[:, s % 2, c, :],
                                                   ident[0:NP, 0:NP])
                    last.then_inc(turned, 1)

                def multiply(i, s):
                    pe.wait_ge(h_t_ready, i * 4 + (s + step0 + 1))
                    for c in range(C4):
                        turned_c = h_t[:, s % 2, c * NP:(c + 1) * NP]
                        if first:
                            pe.wait_ge(banks_free, i * (4 * C4) + (s * C4 + c + 1))
                            nc.tensor.matmul(bank[c % 2][0:NP, 0:R * D], turned_c, w_all[:, 0:R * D], start=True, stop=True)
                            nc.tensor.matmul(bank[2 + c % 2][0:NP, 0:D], turned_c, w_all[:, R * D:],
                                             start=True, stop=True).then_inc(projected, 1)
                        else:
                            last = nc.tensor.matmul(bank[s % 2][0:NP, c * D:(c + 1) * D], turned_c, w2_sb[:, :],
                                                    start=True, stop=True)
                    if not first:
                        last.then_inc(projected, 1)

                turn(0, 0)
                with pe.Fori(0, STEPS // 4) as i:
                    for s in range(4):
                        turn(i, s + 1)
                        multiply(i, s)
                multiply(STEPS // 4, 0)

            def sum_group(h, i, per, u):
                W = width[h]
                if u == 0:
                    pe.wait_ge(evacuated, i * per + (BEFORE[h] + u + 1))
                pe.wait_ge(pick_ready, i * per + (BEFORE[h] + u + 1))
                if h == 1:
                    pe.wait_ge(scaled, i * per + (u + 1))
                else:
                    pe.wait_ge(gathered[u % U], slot_rows(h, i, per, u))
                for k in range(K):
                    nc.tensor.matmul(acc[u % 2][0:WIN, 0:W], pick[:, k, :], rows[:, u % U, k, 0:W],
                                     start=(k == 0), stop=False)
                pe.wait_ge(evacuated, i * per + (BEFORE[h] + u + 1))
                pe.sem_inc(paced, 1)
                nc.tensor.matmul(acc[u % 2][0:WIN, 0:W], carry[:, u % U, :], summed[:, (u - 1) % U, 0:W],
                                 start=False, stop=True).then_inc(group_done, 1)

            def general_hop(h):
                q = general[h]
                n = (h - q.first) * TILES
                with pe.Fori(0, TILES) as t:
                    pe.wait_ge(q.diag, t + (n + 1))
                    nc.tensor.matmul(bank[0][:, 0:P], ones[:, :], diag[:, :], start=True, stop=True).then_inc(q.dst, 1)
                    pe.wait_ge(q.same, t + (n + 1))
                    pe.wait_ge(g_rows[h], t * 16 + 16)
                    nc.tensor.matmul(bank[1][:, 0:width[h]], same_w[:, :], grow[:, 0:width[h]], start=True, stop=True
                                     ).then_inc(q.sum, 1)

            fast = None
            for h in range(HOPS):
                if h == 0:
                    pe.wait_ge(rec_key, 1)
                    for j in range(CH):
                        if j >= 2:
                            pe.wait_ge(rec_back, j - 1)
                        for f in range(FIRST_FIELDS):
                            last = nc.tensor.transpose(bank[j % 2][:, f * P:(f + 1) * P], rec_all[:, j, f, :], ident[:, :])
                        last.then_inc(rec_turned, 1)
                    nc.tensor.matmul(bank[2][0:1, 0:1], ones[:, 0:1], mins[:, 3:4], start=True, stop=True
                                     ).then_inc(ok_sum, 1)
                    pe.wait_ge(setup, 1)
                    fast = pe.value_load(flag[0:1, 0:1], min_val=0, max_val=1)
                if h == 2:
                    pe.wait_ge(gate_in, 16 * CH)
                    for j in range(CH // 4):
                        if j >= 2:
                            pe.wait_ge(gate_back, j - 1)
                        for t in range(4):
                            last = nc.tensor.transpose(bank[j % 2][:, t * P:(t + 1) * P], rec_gate[:, 4 * j + t, :],
                                                       ident[:, :])
                        last.then_inc(gate_turned, 1)
                    pe.wait_ge(gate_back, CH // 4)
                if h not in HYBRID:
                    with pe.If(fast == 1):
                        with pe.Fori(0, IT) as i:
                            for u in range(U):
                                sum_group(h, i, U, u)
                    with pe.Else():
                        general_hop(h)
                else:
                    with pe.If(fast == 1):
                        hh = HYBRID.index(h)
                        pe.wait_ge(table_ready, h + 1)
                        with pe.Fori(0, ITH) as i:
                            for s in range(S):
                                b, q = s // U, s % U
                                if q == 0:
                                    pe.wait_ge(a_there, i * (2 * QUADS) + (HOP_QUADS * hh + QUADS * b + 2))
                                columns = list(range(q * NC // U, (q + 1) * NC // U))
                                first = sum(STEP_PAIRS[:q]) // 2
                                quads = STEP_PAIRS[q] // 2
                                for j in range(first, first + quads):
                                    part = slice((j - first) * len(columns) // quads, (j - first + 1) * len(columns) // quads)
                                    for c in columns[part]:
                                        last = nc.tensor.matmul(d_acc[b][0:D, 0:BN], hs[:, c, :], a_blk[1 - b][:, c, :],
                                                                start=(c == 0), stop=(c == NC - 1))
                                    if q == U - 1 and j == first + quads - 1:
                                        last.then_inc(applied, 1)
                                    if j == first:
                                        pe.wait_ge(hot_ready, i * S + (S * ITH * hh + s + 1))
                                    pe.wait_ge(a_there, i * (2 * QUADS) + (HOP_QUADS * hh + QUADS * b + j + 1))
                                    for t in range(2):
                                        w = 2 * (j - first) + t
                                        last = nc.tensor.matmul(build[j % 2][0:NP, t * 2 * NC:(t + 1) * 2 * NC],
                                                                hot_row[:, s % 2, w, :], hot_key[:, s % 2, w, :],
                                                                start=True, stop=True)
                                    last.then_inc(built, 1)
                                sum_group(h, i, S, s)
                                if q == U - 1:
                                    pe.wait_ge(d_t_ready, i * 2 + (2 * ITH * hh + b + 1))
                                    pe.sem_inc(paced, 1)
                                    nc.tensor.transpose(d_back[0:BN, 0:D], d_t[:, :], ident[0:D, 0:D]).then_inc(d_turned, 1)
                    with pe.Else():
                        general_hop(h)
                if h == 0:
                    project(True)
                if h == 3:
                    project(False)

        @block.vector
        def _(dve):
            made = [0]

            def link(ins):
                made[0] += 1
                ins.then_inc(v, 1)
                dve.wait_ge(v, made[0])

            asked = [0]

            def ask(ins):
                asked[0] += 1
                ins.then_inc(v_out, 1)
                dve.wait_ge(a_out, asked[0])

            def each(ap):
                return ap[:, :].rearrange("p (c o) -> p c o", o=1).to_broadcast([NP, NC, D])

            def each_edge(ap):
                return ap.rearrange("p (g o) -> p g o", o=1).to_broadcast([P, G, K])

            def over_pairs(ap, n):
                return ap.rearrange("p (j o) -> p j o", o=1).to_broadcast([P, CH, n])

            def layernorm():
                link(nc.vector.tensor_reduce(st1[:, :], xs[:, :, :], AX, ALU.add))
                link(nc.vector.tensor_scalar(st2[:, :], st1[:, :], -1.0 / D, None, ALU.mult))
                ask(nc.vector.tensor_tensor(hs[:, :, :], xs[:, :, :], each(st2), ALU.add))
                link(nc.vector.tensor_reduce(st2[:, :], scratch, AX, ALU.add))
                ask(nc.vector.tensor_scalar(st1[:, :], st2[:, :], 1.0 / D, EPS, ALU.mult, ALU.add))
                link(nc.vector.reciprocal(st1[:, :], st2[:, :]))
                return nc.vector.scalar_tensor_tensor(hs[:, :, :], hs[:, :, :], 0.0, each(st1), ALU.max, ALU.mult)

            def floor_div(q, a, d, whole, rest):
                link(nc.vector.tensor_scalar(q, a, 1.0 / d, 0.5 / d - 0.5, ALU.mult, ALU.add))
                link(nc.vector.tensor_copy(whole, q))
                link(nc.vector.tensor_copy(q, whole))
                link(nc.vector.scalar_tensor_tensor(rest, q, -float(d), a, ALU.mult, ALU.add))
                link(nc.vector.tensor_scalar(rest, rest, float(d), None, ALU.is_ge))
                link(nc.vector.tensor_tensor(q, q, rest, ALU.add))

            dve.wait_ge(consts, CONSTS)
            link(nc.vector.tensor_scalar(ident[:, :], iota_row[:, 0:P], iota_col[:, 0:1], None, ALU.is_equal))
            link(nc.vector.tensor_scalar(earlier[:, :], iota_row[:, 0:P], iota_col[:, 0:1], None, ALU.is_lt))
            link(nc.vector.tensor_scalar(same[:, :], iota_row[:, 0:P], 1.0, None, ALU.add))
            link(nc.vector.tensor_scalar(same[:, :], same[:, :], iota_col[:, 0:1], None, ALU.is_equal))
            link(nc.vector.tensor_scalar(diag[:, :], iota_row[:, 0:P], float(1 - P), None, ALU.add))
            link(nc.vector.tensor_scalar(diag[:, :], diag[:, :], iota_col[:, 0:1], None, ALU.is_equal))
            dve.wait_ge(nat_loaded, 32)
            n = EN // NP
            part = [wide[0:NP, t * n:(t + 1) * n] for t in range(4)]
            link(nc.vector.tensor_copy(part[0], wide[0:NP, SRC_AT:DST_AT].bitcast(i32)))
            link(nc.vector.tensor_copy(part[1], wide[0:NP, DST_AT:REL_AT].bitcast(i32)))
            floor_div(part[3], part[0], NC, wide[0:NP, SRC_AT:DST_AT].bitcast(i32), part[2])
            link(nc.vector.tensor_scalar(part[3], part[3], float(NC), None, ALU.mult))
            link(nc.vector.tensor_tensor(part[2], part[0], part[3], ALU.subtract))
            link(nc.vector.scalar_tensor_tensor(wide[0:NP, SRC_AT:DST_AT], part[1], float(NC), part[2],
                                                ALU.mult, ALU.add))
            dve.sem_inc(nat_ready, 1)
            dve.wait_ge(loaded, 16 * LOADS)
            link(nc.vector.tensor_copy(base_row[0:1, 0:G], base_i[0:1, :]))
            link(nc.vector.memset(base_row[0:1, 0:1], 0.0))
            link(nc.vector.tensor_scalar(base_row[0:1, G:G + 1], base_row[0:1, G - 1:G], float(WIN - 1), None, ALU.add))
            link(nc.vector.tensor_copy(base_i[0:1, :], base_row[0:1, 0:G]))
            dve.sem_inc(base_f, 1)
            dve.wait_ge(base_b, 1)
            nc.vector.tensor_copy(base[:, 0:512], bank[0][:, 0:512])
            link(nc.vector.tensor_copy(base[:, 512:G + 1], bank[1][:, 0:G + 1 - 512]))
            link(nc.vector.tensor_copy(wide[:, 0:G * K], off[:, :].bitcast(i32)))
            wide_g = wide[:, 0:G * K].rearrange("p (g k) -> p g k", k=K)
            link(nc.vector.tensor_tensor(off_g, wide_g, each_edge(base[:, 0:G]), ALU.subtract))
            link(nc.vector.tensor_tensor(delta[:, :], base[:, 1:G + 1], base[:, 0:G], ALU.subtract))
            nc.vector.memset(carry_at[:, 0:1], -1.0)
            link(nc.vector.tensor_copy(carry_at[:, 1:G], delta[:, 0:G - 1]))
            link(nc.vector.tensor_tensor(wide_g, each_edge(delta[:, :]), off_g, ALU.subtract))
            link(nc.vector.tensor_reduce(mins[:, 0:1], wide[:, 0:G * K], AX, ALU.min))
            link(nc.vector.tensor_reduce(mins[:, 1:2], off[:, :], AX, ALU.min))
            link(nc.vector.tensor_reduce(mins[:, 2:3], delta[:, :], AX, ALU.max))
            link(nc.vector.tensor_tensor(mins[:, 0:1], mins[:, 0:1], mins[:, 1:2], ALU.min))
            link(nc.vector.tensor_scalar(mins[:, 2:3], mins[:, 2:3], float(WIN - 1), None, ALU.is_le))
            link(nc.vector.scalar_tensor_tensor(mins[:, 0:1], mins[:, 0:1], 0.0, mins[:, 2:3], ALU.is_ge, ALU.mult))
            link(nc.vector.scalar_tensor_tensor(mins[:, 3:4], base[:, G - 1:G], float(N - WIN), mins[:, 0:1],
                                                ALU.is_ge, ALU.mult))
            dve.wait_ge(nat_stored, 32)
            layernorm().then_inc(rows_ready, 1)
            types = wide[:, REL_AT:REL_AT + G * K].bitcast(i32)
            link(nc.vector.tensor_copy(wide[:, 0:G * K], types))
            link(nc.vector.tensor_copy(wide[:, G * K:2 * G * K], idx_all[:, 0:G * K]))
            link(nc.vector.scalar_tensor_tensor(wide[:, 0:G * K], wide[:, 0:G * K], float(N), wide[:, G * K:2 * G * K],
                                                ALU.mult, ALU.add))
            link(nc.vector.tensor_copy(types, wide[:, 0:G * K]))
            dve.sem_inc(rel_ready, 1)
            dve.wait_ge(nat_stored, 48)
            below = wide[:, 0:CH * G].rearrange("p (j g) -> p j g", g=G)
            base_j = base[:, 0:G].rearrange("p (o g) -> p o g", o=1).to_broadcast([P, CH, G])
            link(nc.vector.tensor_tensor(below, base_j, over_pairs(node0[:, :], G), ALU.is_lt))
            link(nc.vector.tensor_reduce(rest20[:, :], below, AX, ALU.add))
            link(nc.vector.tensor_scalar(rest20[:, :], rest20[:, :], -1.0, 0.0, ALU.add, ALU.max))
            link(nc.vector.tensor_copy(rec_i[:, :], rest20[:, :]))
            dve.sem_inc(group_idx, 1)
            dve.wait_ge(groups_in, 16 * CH)
            link(nc.vector.tensor_copy(dst_of, dst_of.bitcast(i32)))
            groups_f = dst_of.rearrange("p (j e) -> p j e", e=GE)
            link(nc.vector.tensor_tensor(groups_f, groups_f, over_pairs(node0[:, :], GE), ALU.is_lt))
            link(nc.vector.tensor_reduce(tmp20[:, :], groups_f, AX, ALU.add))
            link(nc.vector.memset(begins[:, CH:CH + 1], 0.0))
            link(nc.vector.scalar_tensor_tensor(begins[:, 0:CH], rest20[:, :], float(GE), tmp20[:, :], ALU.mult, ALU.add))
            dve.sem_inc(starts, 1)
            floor_div(tmp20[:, :], begins[:, 0:CH], ALIGN, rec_i[:, :], rest20[:, :])
            link(nc.vector.tensor_scalar(rec_i[:, :], tmp20[:, :], float(REC_ROWS - 1), None, ALU.min))
            dve.sem_inc(rec_idx, 1)
            dve.wait_ge(ends_in, 1)
            link(nc.vector.tensor_tensor(edges[:, :], bank[2][:, 0:CH], begins[:, 0:CH], ALU.subtract))
            dve.wait_ge(rec_in, 16 * CH)
            keys = rec_all[:, :, 0, :]
            inside = wide[:, CH * FIRST_FIELDS * P:CH * (FIRST_FIELDS + 1) * P].rearrange("p (j e) -> p j e", e=P)
            link(nc.vector.tensor_tensor(keys, keys, over_pairs(key0[:, :], P), ALU.subtract))
            link(nc.vector.tensor_scalar(inside, keys, 0.0, None, ALU.is_ge))
            link(nc.vector.scalar_tensor_tensor(inside, keys, float(2 * NC), inside, ALU.is_lt, ALU.mult))
            link(nc.vector.tensor_reduce(tmp20[:, :], inside, AX, ALU.add))
            link(nc.vector.tensor_tensor(tmp20[:, :], tmp20[:, :], edges[:, :], ALU.is_equal))
            link(nc.vector.scalar_tensor_tensor(tmp20[:, :], node0[:, :], float(ND), tmp20[:, :], ALU.is_ge, ALU.max))
            link(nc.vector.tensor_reduce(mins[:, 0:1], tmp20[:, :], AX, ALU.min))
            link(nc.vector.scalar_tensor_tensor(mins[:, 0:1], base[:, G0:G0 + 1], float(ND), mins[:, 0:1],
                                                ALU.is_le, ALU.mult))
            link(nc.vector.tensor_tensor(mins[:, 3:4], mins[:, 3:4], mins[:, 0:1], ALU.mult))
            dve.sem_inc(rec_key, 1)
            dve.wait_ge(ok_sum, 1)
            link(nc.vector.tensor_scalar(flag[0:1, 0:1], bank[2][0:1, 0:1], P - 0.5, None, ALU.is_ge))
            dve.sem_inc(setup, 1)
            fast = dve.value_load(flag[0:1, 0:1], min_val=0, max_val=1)
            dve.wait_ge(rec_stored, 16 * CH)

            def products(i):
                dve.wait_ge(attr_in, i * 16 + 16)
                ps = ps_b[:, :].rearrange("p (o f) -> p o f", o=1).to_broadcast([P, U * K, D])
                features = attr[:, :, :].rearrange("p u (k f) -> p (u k) f", f=D)
                nc.vector.tensor_tensor(features, features, ps, ALU.mult).then_inc(prod_ready, 1)
                dve.wait_ge(prod_ready, i + 1)
                nc.vector.tensor_reduce(z25[:, :], features, AX, ALU.add).then_inc(attr_used, 1)
                dve.wait_ge(gate_ready, i + 1)

            def project(first):
                step0 = 0 if first else STEPS

                def take(i, s):
                    dve.wait_ge(turned, i * 4 + (s + step0 + 3))
                    nc.vector.tensor_copy(h_t[:, s % 2, :], bank[6 + s % 2][0:D, 0:C4 * NP]).then_inc(h_t_ready, 1)

                def add(i, s):
                    if first:
                        dve.wait_ge(proj_free, i * 4 + (s + 1))
                        bias = hb_b[:, :].rearrange("p (o f) -> p o f", o=1).to_broadcast([NP, R, D])
                        for c in range(C4):
                            dve.wait_ge(projected, i * (4 * C4) + (s * C4 + c + 1))
                            last = nc.vector.tensor_tensor(proj_sb[s][:, :, c, :],
                                                           bank[c % 2][0:NP, 0:R * D].rearrange("p (r f) -> p r f", f=D),
                                                           bias, ALU.add)
                            if c == C4 - 1:
                                last.then_inc(proj_ready, 1)
                            col = xs[:, bass.ds(i * (4 * C4) + (s * C4 + c), 1), :].rearrange("p c f -> p (c f)")
                            nc.vector.tensor_tensor(col, col, bank[2 + c % 2][0:NP, 0:D], ALU.add).then_inc(banks_free, 1)
                    else:
                        dve.wait_ge(projected, i * 4 + (s + C4 * STEPS + 1))
                        bias = b2_b[:, :].rearrange("p (o f) -> p o f", o=1).to_broadcast([NP, C4, D])
                        z = bank[s % 2][0:NP, 0:C4 * D].rearrange("p (c f) -> p c f", f=D)
                        nc.vector.tensor_tensor(scratch[:, bass.ds(i * (4 * C4) + s * C4, C4), :], z, bias, ALU.add
                                                ).then_inc(z_ready, 1)

                take(0, 0)
                with dve.Fori(0, STEPS // 4) as i:
                    for s in range(4):
                        take(i, s + 1)
                        add(i, s)
                add(STEPS // 4, 0)
                if first:
                    dve.wait_ge(proj_free, STEPS + 4)
                else:
                    dve.wait_ge(z_ready, STEPS)

            def picks(h, i, per, u):
                at = FIRST[h] * K
                dve.wait_ge(group_done, i * per + (BEFORE[h] + u + U))
                nc.vector.tensor_scalar(carry[:, u % U, 0:1], iota_col[0:WIN, :],
                                        carry_at[0:WIN, bass.ds(i * per + (FIRST[h] + u), 1)], None, ALU.is_equal)
                if h == 1:
                    nc.vector.tensor_copy(rows[:, u % U, :, D], gcn_w[:, bass.ds(i * (per * K) + u * K, K)])
                for k in range(K):
                    col = bass.ds(i * (per * K) + (at + u * K + k), 1)
                    if weighted[h]:
                        last = nc.vector.tensor_scalar(pick[:, k, :], iota_row[:, 0:WIN], off[:, col], weight[:, col],
                                                       ALU.is_equal, ALU.mult)
                    else:
                        last = nc.vector.tensor_scalar(pick[:, k, :], iota_row[:, 0:WIN], off[:, col], None,
                                                       ALU.is_equal)
                last.then_inc(pick_ready, 1)
                dve.wait_ge(gathered[u % U], slot_rows(h, i, per, u))
                slot = (u % U) * K
                nc.vector.tensor_copy(idx_now[:, slot:slot + K],
                                      idx_all[:, bass.ds(i * (per * K) + (at + (u + U) * K), K)]).then_inc(idx_ready, 1)
                if h == 1:
                    w = weight[:, bass.ds(i * (per * K) + u * K, K)].rearrange("p (k o) -> p k o", o=1)
                    nc.vector.tensor_tensor(rows[:, u % U, :, 0:D], rows[:, u % U, :, 0:D], w.to_broadcast([P, K, D]),
                                            ALU.mult).then_inc(scaled, 1)

            def first_indices(h):
                at = FIRST[h] * K
                nc.vector.tensor_copy(idx_now[:, :], idx_all[:, at:at + U * K]).then_inc(idx_ready, U)

            def general_hop(h):
                q = general[h]
                nc.vector.memset(wide[:, 0:NC * (D + 1)], 0.0).then_inc(q.zeroed, 1)
                if h == 1:
                    with dve.Fori(0, IT) as i:
                        products(i)
                with dve.Fori(0, G) as g:
                    for k in range(K):
                        n = (h - q.first) * TILES + k
                        dve.wait_ge(q.free, g * K + n + 1)
                        col = bass.ds(g * K + k, 1)
                        nc.vector.tensor_copy(gidx[:, :], idx_all[:, col]).then_inc(q.idx, 1)
                        if h == 1:
                            nc.vector.tensor_copy(grow[:, D:D + 1], gcn_w[:, col])
                        chain = 0

                        def step(ins):
                            nonlocal chain
                            chain += 1
                            ins.then_inc(q.v, 1)
                            dve.wait_ge(q.v, g * (CHAIN * K) + CHAIN * n + chain)

                        step(nc.vector.tensor_tensor(dcol[:, 0:1], off[:, col], base[:, bass.ds(g, 1)], ALU.add))
                        nc.vector.tensor_scalar(diag[:, :], ident[:, :], dcol[:, 0:1], None, ALU.mult).then_inc(q.diag, 1)
                        dve.wait_ge(q.dst, g * K + n + 1)
                        step(nc.vector.tensor_scalar(same[:, :], bank[0][:, 0:P], dcol[:, 0:1], None, ALU.is_equal))
                        w = weight[:, col] if weighted[h] else 1.0
                        step(nc.vector.tensor_scalar(same_w[:, :], same[:, :], w, None, ALU.mult))
                        step(nc.vector.tensor_tensor(diag[:, :], same[:, :], earlier[:, :], ALU.mult))
                        step(nc.vector.tensor_reduce(dcol[:, 1:2], diag[:, :], AX, ALU.add))
                        step(nc.vector.tensor_scalar(dcol[:, 1:2], dcol[:, 1:2], 0.0, None, ALU.is_equal))
                        step(nc.vector.scalar_tensor_tensor(dcol[:, 1:2], dcol[:, 0:1], spare[:, 0:1], dcol[:, 1:2],
                                                            ALU.subtract, ALU.mult))
                        assert chain == CHAIN
                        if h == 1:
                            dve.wait_ge(g_rows[h], g * (16 * K) + 16 * (k + 1))
                            nc.vector.tensor_scalar(grow[:, 0:D], grow[:, 0:D], weight[:, col], None, ALU.mult)
                        nc.vector.tensor_tensor(didx[:, :], dcol[:, 1:2], spare[:, :], ALU.add).then_inc(q.same, 1)

            loads = agg_loads = 0
            for h in range(HOPS):
                loads += {1: 32, 2: 32, 4: 16}.get(h, 0)
                if loads:
                    dve.wait_ge(edge_in, loads)
                if h not in HYBRID:
                    with dve.If(fast == 1):
                        first_indices(h)
                        with dve.Fori(0, IT) as i:
                            products(i)
                            for u in range(U):
                                picks(h, i, U, u)
                    with dve.Else():
                        general_hop(h)
                else:
                    with dve.If(fast == 1):
                        hh = HYBRID.index(h)
                        w_field = 2 if h < 4 else 3
                        first_indices(h)
                        with dve.Fori(0, ITH) as i:
                            for s in range(S):
                                b, q = s // U, s % U
                                if q == 0:
                                    dve.wait_ge(rec_load[b], i * 16 + 16 * ((ITH + 1) * hh + 1))
                                used = QUADS * b + sum(STEP_PAIRS[:q]) // 2 - STEP_PAIRS[q - 1] // 2
                                dve.wait_ge(built, i * (2 * QUADS) + (HOP_QUADS * hh + used + BUILT))
                                first = sum(STEP_PAIRS[:q])
                                for w in range(STEP_PAIRS[q]):
                                    def field(f):
                                        return rec[:, b, f, first + w:first + w + 1]
                                    nc.vector.tensor_scalar(hot_row[:, s % 2, w, :], iota_nc[:, :], field(1), None,
                                                            ALU.is_equal)
                                    if weighted[h]:
                                        last = nc.vector.tensor_scalar(hot_key[:, s % 2, w, :], iota_row[:, :],
                                                                       field(0), field(w_field), ALU.is_equal, ALU.mult)
                                    else:
                                        last = nc.vector.tensor_scalar(hot_key[:, s % 2, w, :], iota_row[:, :],
                                                                       field(0), None, ALU.is_equal)
                                last.then_inc(hot_ready, 1)
                                picks(h, i, S, s)
                    with dve.Else():
                        general_hop(h)

                agg_loads += 32 if h in HYBRID else 16
                dve.wait_ge(agg_in, agg_loads)
                sums = agg_sb[h][:, :, 0:D]
                if h == 0:
                    link(nc.vector.tensor_tensor(xs[:, :, :], xs[:, :, :], sums, ALU.add))
                    layernorm().then_inc(node_ready, 1)
                    project(True)
                elif h == 1:
                    link(nc.vector.tensor_tensor(xs[:, :, :], xs[:, :, :], sums, ALU.add))
                    link(nc.vector.tensor_scalar(deg[:, :], agg_sb[1][:, :, D], 1.0, None, ALU.add))
                    link(nc.vector.tensor_scalar(dinv2[:, :], deg[:, :], 0.0, None, ALU.is_gt))
                    ask(nc.vector.tensor_scalar(deg[:, :], deg[:, :], 1.2e-38, None, ALU.max))
                    link(nc.vector.reciprocal(dinv[:, :], dinv[:, :]))
                    link(nc.vector.tensor_tensor(dinv[:, :], dinv[:, :], dinv2[:, :], ALU.mult))
                    link(nc.vector.tensor_tensor(dinv2[:, :], dinv[:, :], dinv[:, :], ALU.mult))
                    link(layernorm())
                    nc.vector.tensor_tensor(hs[:, :, :], hs[:, :, :], each(dinv), ALU.mult).then_inc(rows_ready, 1)
                elif h == 2:
                    link(nc.vector.tensor_tensor(hs[:, :, :], hs[:, :, :], sums, ALU.add))
                    nc.vector.tensor_tensor(hs[:, :, :], hs[:, :, :], each(dinv2), ALU.mult).then_inc(rows_ready, 1)
                elif h == 3:
                    link(nc.vector.tensor_tensor(hs[:, :, :], hs[:, :, :], sums, ALU.add))
                    nc.vector.tensor_tensor(hs[:, :, :], hs[:, :, :], each(dinv), ALU.mult).then_inc(node_ready, 1)
                    project(False)
                    ask(nc.vector.tensor_scalar(hs[:, :, :], scratch, 0.0, None, ALU.min))
                    link(nc.vector.tensor_scalar(scratch, scratch, 0.0, None, ALU.max))
                    link(nc.vector.scalar_tensor_tensor(scratch, hs[:, :, :], -1.0, scratch, ALU.add, ALU.add))
                    link(nc.vector.tensor_tensor(xs[:, :, :], xs[:, :, :], scratch, ALU.add))
                    link(layernorm())
                    nc.vector.tensor_tensor(hs[:, :, :], hs[:, :, :], each(cj_sb), ALU.mult).then_inc(rows_ready, 1)
                else:
                    link(nc.vector.tensor_tensor(sums, sums, each(ci_sb), ALU.mult))
                    nc.vector.tensor_tensor(xs[:, :, :], xs[:, :, :], sums, ALU.add).then_inc(rows_ready, 1)


_INS = ["x", "src", "dst", "src_nat", "dst_nat", "w_nat", "etype", "edge_attr", "edge_w", "att", "cj", "ci",
        "rel_w", "h_bias", "loop_w", "w_t", "b2", "ps_w"]


def kernel(x, src, dst, edge_attr_64, edge_type_8, edge_weight, edge_weight1, node_vec1, node_vec1_n2,
           L1_gnn_weight, L1_gnn_h_bias, L1_gnn_loop_weight, L2_gnn_W, L2_gnn_b, L3_gnn_ps_w):
    import numpy as np
    import concourse.bacc as bacc
    from concourse.bass_utils import run_bass_kernel_spmd

    def by_edge(a):
        return np.ascontiguousarray(np.asarray(a).reshape(G, P, K).transpose(1, 0, 2).reshape(P, G * K))

    arrays = {
        "x": x, "src": by_edge(src), "dst": by_edge(dst),
        "src_nat": src, "dst_nat": dst, "w_nat": edge_weight,
        "etype": by_edge(edge_type_8),
        "edge_attr": edge_attr_64, "edge_w": by_edge(edge_weight), "att": by_edge(edge_weight1),
        "cj": node_vec1, "ci": node_vec1_n2, "rel_w": L1_gnn_weight, "h_bias": L1_gnn_h_bias,
        "loop_w": L1_gnn_loop_weight, "w_t": np.asarray(L2_gnn_W).T, "b2": L2_gnn_b, "ps_w": L3_gnn_ps_w,
    }
    arrays = {f"in_{n}": np.ascontiguousarray(arrays[n]) for n in _INS}
    nc = bacc.Bacc("TRN2", target_bir_lowering=False, num_devices=1)
    args = [nc.dram_tensor(n, a.shape, mybir.dt.from_np(a.dtype), kind="ExternalInput").ap() for n, a in arrays.items()]
    out = nc.dram_tensor("out_x", (N, D), mybir.dt.float32, kind="ExternalOutput").ap()
    gnn_kernel(nc, *args, out)
    r = run_bass_kernel_spmd(nc, [arrays], core_ids=[0])
    return r.results[0]["out_x"]
```
